# Optimizing a Trainium2 kernel written in Bass

```python
import numpy as np
import jax
import jax.numpy as jnp

def _softmax(x, axis=-1):
    return jax.nn.softmax(x, axis=axis)

def _gelu(x):
    return jax.nn.gelu(x, approximate=True)

def _silu(x):
    return jax.nn.silu(x)

def _sigmoid(x):
    return jax.nn.sigmoid(x)

def _layernorm(x, axis=-1, eps=1e-05):
    m = jnp.mean(x, axis=axis, keepdims=True)
    v = jnp.var(x, axis=axis, keepdims=True)
    return (x - m) / jnp.sqrt(v + eps)

def _scatter_add(tgt, idx, src, axis=0):
    return tgt.at[idx].add(src)

def _segment_sum(src, seg, n):
    return jax.ops.segment_sum(src, seg, n)
kernel_name = 'mk_adaln_ffn_d2_seqx_r4_bd91c2'

def setup_inputs(seed: int=0):
    np.random.seed(seed)
    _w = jnp.asarray

    def _rec_inputs():
        import jax
        import jax.numpy as jnp
        _rk = jax.random.key(seed)
        x = -0.000125 + 0.9999 * jax.random.normal(jax.random.fold_in(_rk, 1), (128, 64, 1024), jnp.float32)
        _lenS = 64 - jax.random.randint(jax.random.fold_in(_rk, 7), (128,), 0, max(1, 64 // 4) + 1, jnp.int32)
        _lenS2 = 64 - jax.random.randint(jax.random.fold_in(_rk, 8), (128,), 0, max(1, 64 // 4) + 1, jnp.int32)
        cond_128 = 0.0061147 + 1.02565 * jax.random.normal(jax.random.fold_in(_rk, 11), (128, 128), jnp.float32)
        fside_S_0 = -0.022604 + 0.987366 * jax.random.normal(jax.random.fold_in(_rk, 12), (64,), jnp.float32)
        return (x, cond_128, fside_S_0)
    x, cond_128, fside_S_0 = _rec_inputs()

    def _L0_cond_setup():
        import jax, jax.numpy as jnp
        import numpy as np
        K = 8
        T = 1.0
        D_EMBD = 128
        IN_C = 64
        OUT_C = 64
        BS = 32
        H = 1024
        HID = 128
        key = jax.random.key(seed)
        ks = jax.random.split(key, 10)
        s = lambda fan_in: 1.0 / np.sqrt(fan_in)
        return {'x': jax.random.normal(ks[0], (BS, IN_C, H), dtype=jnp.float32), 'embedding': jax.random.normal(ks[1], (BS, D_EMBD), dtype=jnp.float32), 'W0': jax.random.normal(ks[2], (D_EMBD, HID), dtype=jnp.float32) * s(D_EMBD), 'b0': jnp.zeros((HID,), dtype=jnp.float32), 'W1': jax.random.normal(ks[3], (HID, HID), dtype=jnp.float32) * s(HID), 'b1': jnp.zeros((HID,), dtype=jnp.float32), 'W2': jax.random.normal(ks[4], (HID, K), dtype=jnp.float32) * s(HID), 'b2': jnp.zeros((K,), dtype=jnp.float32), 'weight': jax.random.normal(ks[5], (K, OUT_C, IN_C, 1), dtype=jnp.float32) * s(IN_C), 'bias_k': jax.random.normal(ks[6], (K, OUT_C), dtype=jnp.float32) * 0.1}
    _L0_cond_all = _L0_cond_setup()
    _L0_cond_in = {k: v for k, v in _L0_cond_all.items() if k in ('W0', 'b0', 'W1', 'b1', 'W2', 'b2', 'weight', 'bias_k')}
    del _L0_cond_all

    def _L0_ffn_setup():
        import jax, jax.numpy as jnp
        import numpy as np
        MAX_THRESHOLD = 1.0 / 8.0
        SCALING = 32.0 / 16.0
        key = jax.random.key(seed)
        ks = jax.random.split(key, 8)
        B_, S, D, O, E, R = (4, 512, 1024, 1024, 8, 16)
        sd = 1.0 / np.sqrt(D)
        return {'x': jax.random.normal(ks[0], (B_, S, D), jnp.float32), 'W_base': jax.random.normal(ks[1], (O, D), jnp.float32) * sd, 'b_base': jax.random.normal(ks[2], (O,), jnp.float32) * 0.01, 'W_gate': jax.random.normal(ks[3], (E, D), jnp.float32) * sd, 'W_thr': jax.random.normal(ks[4], (1, D), jnp.float32) * sd, 'b_thr': jax.random.normal(ks[5], (1,), jnp.float32) * 0.01, 'A': jax.random.normal(ks[6], (E, R, D), jnp.float32) * sd, 'B': jax.random.normal(ks[7], (O,), jnp.float32)[None, :, None] * jnp.zeros((E, O, R), jnp.float32) + jax.random.normal(jax.random.fold_in(key, 7), (E, O, R), jnp.float32) * (1.0 / np.sqrt(R))}
    _L0_ffn_all = _L0_ffn_setup()
    _L0_ffn_in = {k: v for k, v in _L0_ffn_all.items() if k in ('W_base', 'b_base', 'W_gate', 'W_thr', 'b_thr', 'A', 'B')}
    del _L0_ffn_all

    def _L1_cond_setup():
        import jax, jax.numpy as jnp
        import numpy as np
        from jax import lax
        N, C_IN, L = (32, 64, 1024)
        C_OUT, K, GROUPS = (64, 9, 4)
        C_DIM, PAD, STRIDE = (128, 4, 1)
        key = jax.random.key(seed)
        k1, k2, k3, k4, k5 = jax.random.split(key, 5)
        x = jax.random.normal(k1, (N, C_IN, L), dtype=jnp.float32)
        c = jax.random.normal(k2, (N, C_DIM), dtype=jnp.float32)
        weight = jax.random.normal(k3, (C_OUT, C_IN // GROUPS, K), dtype=jnp.float32)
        c_weight = jax.random.normal(k4, (C_OUT, C_DIM), dtype=jnp.float32)
        bias = jax.random.normal(k5, (C_OUT,), dtype=jnp.float32)
        return {'x': x, 'c': c, 'weight': weight, 'c_weight': c_weight, 'bias': bias}
    _L1_cond_all = _L1_cond_setup()
    _L1_cond_in = {k: v for k, v in _L1_cond_all.items() if k in ('weight', 'c_weight')}
    del _L1_cond_all

    def _L1_ffn_setup():
        import jax, jax.numpy as jnp
        import numpy as np
        B, S, D_IN, D_OUT = (2, 512, 1024, 1024)
        E, K, R = (8, 2, 16)
        SCALING = 32.0 / 16.0
        key = jax.random.key(seed)
        ks = jax.random.split(key, 6)
        x = jax.random.normal(ks[0], (B, S, D_IN), dtype=jnp.float32)
        gate_w = jax.random.normal(ks[1], (E, D_IN), dtype=jnp.float32) * 0.02
        base_w = jax.random.normal(ks[2], (D_OUT, D_IN), dtype=jnp.float32) * 0.02
        base_b = jax.random.normal(ks[3], (D_OUT,), dtype=jnp.float32) * 0.02
        lora_A = jax.random.normal(ks[4], (E, R, D_IN), dtype=jnp.float32) * 0.02
        lora_B = jax.random.normal(ks[5], (E, D_OUT, R), dtype=jnp.float32) * 0.02
        return {'x': x, 'gate_w': gate_w, 'base_w': base_w, 'base_b': base_b, 'lora_A': lora_A, 'lora_B': lora_B}
    _L1_ffn_all = _L1_ffn_setup()
    _L1_ffn_in = {k: v for k, v in _L1_ffn_all.items() if k in ('gate_w', 'base_w', 'base_b', 'lora_A', 'lora_B')}
    del _L1_ffn_all
    return {'x': x, 'cond_128': cond_128, 'fside_S_0': fside_S_0, 'L0_cond_W0': _L0_cond_in['W0'], 'L0_cond_b0': _L0_cond_in['b0'], 'L0_cond_W1': _L0_cond_in['W1'], 'L0_cond_b1': _L0_cond_in['b1'], 'L0_cond_W2': _L0_cond_in['W2'], 'L0_cond_b2': _L0_cond_in['b2'], 'L0_cond_weight': _L0_cond_in['weight'], 'L0_cond_bias_k': _L0_cond_in['bias_k'], 'L0_ffn_W_base': _L0_ffn_in['W_base'], 'L0_ffn_b_base': _L0_ffn_in['b_base'], 'L0_ffn_W_gate': _L0_ffn_in['W_gate'], 'L0_ffn_W_thr': _L0_ffn_in['W_thr'], 'L0_ffn_b_thr': _L0_ffn_in['b_thr'], 'L0_ffn_A': _L0_ffn_in['A'], 'L0_ffn_B': _L0_ffn_in['B'], 'L1_cond_weight': _L1_cond_in['weight'], 'L1_cond_c_weight': _L1_cond_in['c_weight'], 'L1_ffn_gate_w': _L1_ffn_in['gate_w'], 'L1_ffn_base_w': _L1_ffn_in['base_w'], 'L1_ffn_base_b': _L1_ffn_in['base_b'], 'L1_ffn_lora_A': _L1_ffn_in['lora_A'], 'L1_ffn_lora_B': _L1_ffn_in['lora_B']}

def reference(x, cond_128, fside_S_0, L0_cond_W0, L0_cond_b0, L0_cond_W1, L0_cond_b1, L0_cond_W2, L0_cond_b2, L0_cond_weight, L0_cond_bias_k, L0_ffn_W_base, L0_ffn_b_base, L0_ffn_W_gate, L0_ffn_W_thr, L0_ffn_b_thr, L0_ffn_A, L0_ffn_B, L1_cond_weight, L1_cond_c_weight, L1_ffn_gate_w, L1_ffn_base_w, L1_ffn_base_b, L1_ffn_lora_A, L1_ffn_lora_B):
    import jax
    import jax.numpy as jnp

    def _L0_cond_ref(x, embedding, W0, b0, W1, b1, W2, b2, weight, bias_k):
        import jax, jax.numpy as jnp
        import numpy as np
        K = 8
        T = 1.0
        D_EMBD = 128
        IN_C = 64
        OUT_C = 64
        BS = 32
        H = 1024
        HID = 128
        h = jax.nn.gelu(embedding @ W0 + b0, approximate=False)
        h = jax.nn.gelu(h @ W1 + b1, approximate=False)
        att = jax.nn.softmax((h @ W2 + b2) / T, axis=-1)
        agg_w = jnp.einsum('bk,koi->boi', att, weight[..., 0])
        agg_b = att @ bias_k
        out = jnp.einsum('boi,bih->boh', agg_w, x) + agg_b[:, :, None]
        return out

    def _L0_ffn_ref(x, W_base, b_base, W_gate, W_thr, b_thr, A, B):
        import jax, jax.numpy as jnp
        import numpy as np
        MAX_THRESHOLD = 1.0 / 8.0
        SCALING = 32.0 / 16.0
        base = jnp.einsum('bsd,od->bso', x, W_base) + b_base
        D = x.shape[-1]
        xf = x.reshape(-1, D)
        gate_logits = jax.nn.softmax(xf @ W_gate.T, axis=-1)
        thresholds = jax.nn.sigmoid(xf @ W_thr.T + b_thr) * MAX_THRESHOLD
        adapted = gate_logits - thresholds
        selected = (adapted >= 0).astype(x.dtype)
        weights = adapted * selected
        wsum = jnp.sum(weights, axis=-1, keepdims=True)
        wsum = jnp.where(wsum == 0, jnp.ones_like(wsum), wsum)
        weights = weights / wsum
        h = jnp.einsum('nd,erd->ner', xf, A)
        moe = jnp.einsum('ner,ne,eor->no', h, weights, B) * SCALING
        out = base + moe.reshape(base.shape)
        return out

    def _L1_cond_ref(x, c, weight, c_weight, bias):
        import jax, jax.numpy as jnp
        import numpy as np
        from jax import lax
        N, C_IN, L = (32, 64, 1024)
        C_OUT, K, GROUPS = (64, 9, 4)
        C_DIM, PAD, STRIDE = (128, 4, 1)
        out = lax.conv_general_dilated(x, weight, window_strides=(STRIDE,), padding=[(PAD, PAD)], dimension_numbers=('NCH', 'OIH', 'NCH'), feature_group_count=GROUPS)
        ctx = jnp.einsum('nd,od->no', c, c_weight)
        out = out + ctx[:, :, None] + bias[None, :, None]
        return out

    def _L1_ffn_ref(x, gate_w, base_w, base_b, lora_A, lora_B):
        import jax, jax.numpy as jnp
        import numpy as np
        B, S, D_IN, D_OUT = (2, 512, 1024, 1024)
        E, K, R = (8, 2, 16)
        SCALING = 32.0 / 16.0
        gate_logits = jnp.einsum('bsd,ed->bse', x, gate_w)
        weights, selected = jax.lax.top_k(gate_logits, K)
        weights = jax.nn.softmax(weights.astype(jnp.float32), axis=2).astype(x.dtype)
        result = jnp.einsum('bsd,od->bso', x, base_w) + base_b
        w_full = jnp.sum(jax.nn.one_hot(selected, E, dtype=x.dtype) * weights[..., None], axis=2)
        low = jnp.einsum('bsd,erd->ebsr', x, lora_A)
        lora_out = jnp.einsum('ebsr,eor,bse->bso', low, lora_B, w_full)
        result = result + SCALING * lora_out
        return result
    x = x + _L0_ffn_ref(_L0_cond_ref(x, cond_128, L0_cond_W0, L0_cond_b0, L0_cond_W1, L0_cond_b1, L0_cond_W2, L0_cond_b2, L0_cond_weight, L0_cond_bias_k), L0_ffn_W_base, L0_ffn_b_base, L0_ffn_W_gate, L0_ffn_W_thr, L0_ffn_b_thr, L0_ffn_A, L0_ffn_B)
    x = x + _L1_ffn_ref(_L1_cond_ref(x, cond_128, L1_cond_weight, L1_cond_c_weight, fside_S_0), L1_ffn_gate_w, L1_ffn_base_w, L1_ffn_base_b, L1_ffn_lora_A, L1_ffn_lora_B)
    return x

_drawn_inputs = setup_inputs


def setup_inputs(seed=0):
    import zlib

    import numpy as np

    out = dict(_drawn_inputs(seed))
    spreads = {'L0_cond_b0': (0.0, 0.546), 'L0_cond_b1': (0.0, 0.309), 'L0_cond_b2': (0.0, 0.296)}
    factors = {'L0_ffn_b_base': 7.319, 'L1_ffn_base_b': 35.596}
    for name, (base, spread) in spreads.items():
        noise = np.random.default_rng([zlib.crc32(name.encode()), seed]).standard_normal(out[name].shape)
        drawn = base * np.exp(spread * noise) if base else spread * noise
        out[name] = jnp.asarray(drawn.astype(out[name].dtype))
    for name, factor in factors.items():
        out[name] = (out[name] * factor).astype(out[name].dtype)
    return out
```

```python
import concourse.bass as bass
from concourse import mybir
from contextlib import ExitStack

F32 = mybir.dt.float32
F32R = mybir.dt.float32r
U32 = mybir.dt.uint32
ALU = mybir.AluOpType
ACT = mybir.ActivationFunctionType
AX = mybir.AxisListType

P = 128
C = 64
H = 1024
KT = H // P
HB = 512
E_, R_ = 8, 16
ER = E_ * R_
NAG0 = ER + E_ + 2
NAG1 = ER + E_
G, GC = 4, 16
TAPS, PAD = 9, 4
BR = 8
Q = H // BR
BG = P // GC
QP = Q + 2
XW = BG * QP
MODES = 8
CW = 2 * P


def bcast(ap, axis, n):
    v = ap.unsqueeze(axis)
    shape = list(v.shape)
    shape[axis] = n
    return v.broadcast_to(shape)


def build(nc, x, embT, w0, b0, w1, b1, w2, b2, mixw, mixb, l0wT, l0b, l0ag, bthr, l0B,
          convw, cwT, cbias, l1wT, l1b, l1ag, l1B, out):
    NT = x.shape[0]
    STEPS = NT // P
    x1 = nc.dram_tensor("x1_scratch", [NT, H], F32).ap()
    rows = nc.dram_tensor("row_scratch", [2, STEPS, P], F32).ap()
    atts = nc.dram_tensor("att_scratch", [2, STEPS, MODES], F32).ap()

    with ExitStack() as ctx:
        def sb(name, shape, dt=F32):
            return ctx.enter_context(nc.sbuf_tensor(name, shape, dt))

        def sem(name):
            return ctx.enter_context(nc.semaphore(name))

        stage = sb("stage", [P, KT, H])
        Whi, Wlo = sb("Whi", [P, KT, H], F32R), sb("Wlo", [P, KT, H], F32R)
        AG0hi, AG0lo = sb("AG0hi", [P, KT, NAG0], F32R), sb("AG0lo", [P, KT, NAG0], F32R)
        AG1hi, AG1lo = sb("AG1hi", [P, KT, NAG1], F32R), sb("AG1lo", [P, KT, NAG1], F32R)
        Bhi, Blo = sb("Bhi", [P, 2, H], F32R), sb("Blo", [P, 2, H], F32R)
        Chi, Clo = sb("Chi", [P, G, CW], F32R), sb("Clo", [P, G, CW], F32R)
        bias = sb("bias", [P, H])
        Xraw = sb("Xraw", [P, 2, XW])
        Xhi, Xlo = sb("Xhi", [P, XW], F32R), sb("Xlo", [P, XW], F32R)
        Y = sb("Y", [P, H])
        Yhi, Ylo = sb("Yhi", [P, 2, H], F32R), sb("Ylo", [P, 2, H], F32R)
        res = sb("res", [P, 2, H])
        outb = sb("outb", [P, 2, H])
        row = sb("row", [P, 2, P])
        attb = sb("attb", [P, STEPS, MODES])
        mixT = sb("mixT", [P, MODES, C])
        prod = sb("prod", [P, MODES, C])
        agg = sb("agg", [P, C])
        Mhi, Mlo = sb("Mhi", [P, P], F32R), sb("Mlo", [P, P], F32R)
        ag = sb("ag", [P, NAG0])
        hw = sb("hw", [P, P])
        HThi, HTlo = sb("HThi", [P, P], F32R), sb("HTlo", [P, P], F32R)
        ident = sb("ident", [P, P])
        iota = sb("iota", [P, E_])
        small = sb("small", [P, 64])
        idx = sb("idx", [P, E_], U32)
        nmax, den, rec = small[:, 0:1], small[:, 2:4], small[:, 4:6]
        texp, wsum, guard, rguard = small[:, 6:7], small[:, 7:8], small[:, 8:9], small[:, 9:10]
        nbthr, m8 = small[:, 10:11], small[:, 16:24]
        eg, adapted, wrelu, wts = small[:, 24:32], small[:, 32:40], small[:, 40:48], small[:, 48:56]
        diff, idxf, e2, s2, r2 = small[:, 1:2], small[:, 56:58], small[:, 58:59], small[:, 59:60], small[:, 60:61]
        hot2, hot12 = small[:, 24:32], small[:, 32:40]

        psB = ctx.enter_context(nc.psum_tensor("psB", [P, 4, HB], F32))
        psT = ctx.enter_context(nc.psum_tensor("psT", [P, 2, HB], F32))
        psG = ctx.enter_context(nc.psum_tensor("psG", [P, HB], F32))
        psW = ctx.enter_context(nc.psum_tensor("psW", [P, HB], F32))

        h0, h1, emb, w0s, w1s = (Y[:, k * P:(k + 1) * P] for k in range(5))
        w2s, b0s, b1s, cws = Y[:, 640:648], Y[:, 648:649], Y[:, 649:650], Y[:, 656:720]
        b2s, cbs = Y[0:STEPS, 720:736], Y[0:STEPS, 736:800]
        lg, ex, att = (Y[0:STEPS, k:k + 16].rearrange("p (a k) -> p a k", a=2) for k in (800, 816, 832))
        nmx2, sum2, rec2 = Y[0:STEPS, 848:850], Y[0:STEPS, 850:852], Y[0:STEPS, 852:854]
        aprod = outb[0:STEPS, 0, :].rearrange("p (a k o) -> p a k o", a=2, k=MODES)
        mixbs = outb[0:STEPS, 1, 0:MODES * C].rearrange("p (k o) -> p k o", k=MODES)
        arow, crow = outb[0:STEPS, 1, 512:640], outb[0:STEPS, 1, 640:768]
        flat = stage[:, :, :].rearrange("p k n -> p (k n)")
        agraw = flat[:, 0:KT * NAG1].rearrange("p (k n) -> p k n", k=KT)
        b1raw = flat[:, 2048:2048 + H]
        craw = flat[:, 4096:4096 + G * CW].rearrange("p (g n) -> p g n", g=G)
        resflat = res[:, :, :].rearrange("p a n -> p (a n)")
        ag0raw = resflat[:, 0:KT * (NAG0 - 1)].rearrange("p (k n) -> p k n", k=KT)
        b0raw = outb[:, 0, :]

        small_in, mixb_in = sem("small_in"), sem("mixb_in")
        ag0_in, b0_in, bias_in = sem("ag0_in"), sem("b0_in"), sem("bias_in")
        w_in = [sem(f"w_in{k}") for k in range(KT)]
        l1s_in, conv_zero, conv_in = sem("l1s_in"), sem("conv_zero"), sem("conv_in")
        ident_zero, consts = sem("ident_zero"), sem("consts")
        mm_cond, act_cond, dve_cond = sem("mm_cond"), sem("act_cond"), sem("dve_cond")
        cond_out, att_in = sem("cond_out"), sem("att_in")
        w_hi, w_lo, w_loP = sem("w_hi"), sem("w_lo"), sem("w_loP")
        s_hi, s_lo = sem("s_hi"), sem("s_lo")
        base_tile = sem("base_tile")
        x_loaded = [sem(f"x_loaded{p}") for p in range(2)]
        g_loaded = [sem(f"g_loaded{p}") for p in range(2)]
        r_loaded = [sem(f"r_loaded{p}") for p in range(2)]
        row_loaded = [sem(f"row_loaded{p}") for p in range(2)]
        stored = [sem(f"stored{p}") for p in range(2)]
        pad_zero = sem("pad_zero")
        x_hi, x_lo = sem("x_hi"), sem("x_lo")
        prod_ready, agg_ready, m_hi, m_lo = sem("prod_ready"), sem("agg_ready"), sem("m_hi"), sem("m_lo")
        mixed, y_half, yhi_half, ylo_half = sem("mixed"), sem("y_half"), sem("yhi_half"), sem("ylo_half")
        ag_done, ag_copied = sem("ag_done"), sem("ag_copied")
        nmax_ready, exp_ready, gate0 = sem("nmax_ready"), sem("exp_ready"), sem("gate0")
        m8_ready, diff_ready, exp2_ready, gate1 = sem("m8_ready"), sem("diff_ready"), sem("exp2_ready"), sem("gate1")
        hw_ready, tr_done, ht_hi, ht_lo = sem("hw_ready"), sem("tr_done"), sem("ht_hi"), sem("ht_lo")
        wts_ready, up_done = sem("wts_ready"), sem("up_done")
        res_ready, o_done = sem("res_ready"), sem("o_done")

        def as_f32(ap):
            return ap.bitcast(F32)

        def run(eng, step):
            def layer(n):
                return n // STEPS if n < 2 * STEPS else None

            def peeled(n):
                step(n // 2, n % 2, layer(n), layer(n + 1), layer(n + 2))

            for lay in range(2):
                first = lay * STEPS
                peeled(first)
                peeled(first + 1)
                with eng.Fori(first // 2 + 1, (first + STEPS) // 2 - 1) as j:
                    step(j, 0, lay, lay, lay)
                    step(j, 1, lay, lay, lay)
                peeled(first + STEPS - 2)
                peeled(first + STEPS - 1)

        block = ctx.enter_context(nc.Block())

        @block.sync
        def _(sp):
            def load_x(j, par, layer):
                n = 2 * j + par
                if layer == 0:
                    sp.dma_start(Xraw[:, par, 0:H], x[bass.ds(n * P, P), :]).then_inc(x_loaded[par], 16)
                else:
                    dst = Xraw[:, par, :].rearrange("p (b q) -> p b q", b=BG)
                    m = n - STEPS
                    src = x1[bass.ds(m * P, P), :].rearrange("(b i) (r q) -> r i b q", b=BG, r=BR)
                    for r in range(BR):
                        sp.dma_start(dst[r * GC:(r + 1) * GC, :, 1:1 + Q], src[r]).then_inc(g_loaded[par], 16)
                sp.dma_start(row[:, par, :], rows[layer, bass.ds(n - layer * STEPS, 1), :].rearrange("a t -> (a t)")
                             .partition_broadcast(P)).then_inc(row_loaded[par], 16)

            sp.dma_start(Xraw[:, 0, 0:H], x[0:P, :]).then_inc(x_loaded[0], 16)
            sp.dma_start(ag0raw, l0ag.rearrange("(k p) n -> p k n", p=P)).then_inc(ag0_in, 16)
            for k in range(KT):
                sp.dma_start(stage[:, k, :], l0wT[k * P:(k + 1) * P, :]).then_inc(w_in[k], 16)
            sp.dma_start(Xraw[:, 1, 0:H], x[P:2 * P, :]).then_inc(x_loaded[1], 16)
            sp.dma_start(bias[:, :], l0b.partition_broadcast(P)).then_inc(bias_in, 16)
            sp.wait_ge(dve_cond, 4)
            sp.dma_start(atts.rearrange("a s k -> s a k"), att).then_inc(cond_out, 16)
            sp.wait_ge(cond_out, 16)
            for a in range(2):
                sp.dma_start(attb[a * C:(a + 1) * C, :, :].rearrange("p s k -> p (s k)"),
                             atts[a].rearrange("s k -> (s k)").partition_broadcast(C)).then_inc(att_in, 16)
            sp.wait_ge(dve_cond, 6)
            sp.dma_start(b0raw, l0B).then_inc(b0_in, 16)
            sp.dma_start(rows[0], arow).then_inc(cond_out, 16)
            sp.dma_start(rows[1], crow).then_inc(cond_out, 16)
            sp.wait_ge(cond_out, 48)
            for par in range(2):
                sp.dma_start(row[:, par, :], rows[0, par, :].partition_broadcast(P)).then_inc(row_loaded[par], 16)

            def step(j, par, lay, lay1, lay2):
                n = 2 * j + par
                if lay2 is not None:
                    sp.wait_ge(x_hi, n + 1)
                    sp.wait_ge(x_lo, n + 1)
                    if lay == 0:
                        sp.wait_ge(res_ready, n + 1)
                    sp.wait_ge(y_half, 2 * n + 2)
                    if lay2 == 1:
                        if lay == 0:
                            sp.wait_ge(pad_zero, par + 1)
                        sp.wait_ge(stored[par], 16 * (j - STEPS // 2 + 2))
                    load_x(j + 1, par, lay2)
                if lay == 0 and isinstance(j, int) and n == 0:
                    sp.wait_ge(w_hi, KT)
                    sp.wait_ge(w_lo, KT // 2)
                    sp.wait_ge(w_loP, KT // 2)
                    sp.dma_start(agraw, l1ag.rearrange("(p k) n -> p k n", p=P)).then_inc(l1s_in, 16)
                    sp.dma_start(b1raw, l1B).then_inc(l1s_in, 16)
                    sp.wait_ge(conv_zero, 1)
                    for r in range(BR):
                        to = craw[r * GC:(r + 1) * GC, :, :].rearrange("p g (t o) -> p g t o", o=GC)
                        lo, hi = max(0, r - PAD), min(BR - 1, r + PAD)
                        sp.dma_start(to[:, :, lo:hi + 1, :], convw[:, :, lo - r + PAD:hi - r + PAD + 1, :])\
                            .then_inc(conv_in, 16)
                        if r >= PAD:
                            sp.dma_start(to[:, :, BR:BR + r - PAD + 1, :],
                                         convw[:, :, BR + PAD - r:BR + 1, :]).then_inc(conv_in, 16)
                        else:
                            sp.dma_start(to[:, :, BR + r + PAD:BR + 8, :],
                                         convw[:, :, 0:PAD - r, :]).then_inc(conv_in, 16)
                if lay == 0 and isinstance(j, int) and n == 1:
                    sp.wait_ge(s_hi, 5)
                    sp.wait_ge(s_lo, 5)
                    for k in range(KT):
                        sp.dma_start(stage[:, k, :], l1wT.rearrange("(p k) n -> p k n", p=P)[:, k, :])\
                            .then_inc(w_in[k], 16)
                if isinstance(j, int) and n == STEPS - 1:
                    sp.dma_start(bias[:, :], l1b.partition_broadcast(P)).then_inc(bias_in, 16)
                sp.wait_ge(o_done, n + 1)
                to = x1 if lay == 0 else out
                sp.dma_start(to[bass.ds((n - lay * STEPS) * P, P), :], outb[:, par, :]).then_inc(stored[par], 16)
                if lay2 == 1:
                    sp.dma_start(res[:, par, :], x1[bass.ds((n + 2 - STEPS) * P, P), :]).then_inc(r_loaded[par], 16)

            run(sp, step)
            for par in range(2):
                sp.wait_ge(stored[par], 16 * STEPS)

        @block.gpsimd
        def _(pool):
            pool.memset(ident[:, :], 0.0).then_inc(ident_zero, 1)
            pool.wait_ge(ident_zero, 1)
            pool.affine_select(out=ident[:, :], in_=ident[:, :], compare_op=ALU.not_equal, fill=1.0, base=0,
                               pattern=[[-1, P]], channel_multiplier=1).then_inc(consts, 1)
            for e in range(E_):
                last = pool.memset(iota[:, e:e + 1], float(e))
            last.then_inc(consts, 1)
            pool.memset(as_f32(Mhi[:, :]), 0.0)
            pool.memset(as_f32(Mlo[:, :]), 0.0)
            pool.memset(as_f32(AG0hi[:, :, :])[:, :, NAG0 - 1:NAG0], 0.0)
            pool.memset(as_f32(AG0lo[:, :, :])[:, :, NAG0 - 1:NAG0], 0.0).then_inc(consts, 1)

            def split_lo(k, layer):
                pool.wait_ge(w_hi, KT * layer + k + 1)
                pool.tensor_tensor(Wlo[:, k, :], stage[:, k, :], as_f32(Whi[:, k, :]), ALU.subtract)\
                    .then_inc(w_loP, 1)

            for k in range(1, KT, 2):
                split_lo(k, 0)
            pool.wait_ge(bias_in, 16)
            pool.wait_ge(s_lo, 1)

            def residual(j, par, layer):
                n = 2 * j + par
                if layer == 0:
                    pool.wait_ge(x_loaded[par], 16 * (j + 1))
                    if not (isinstance(j, int) and j == 0):
                        pool.wait_ge(o_done, n - 1)
                    pool.tensor_tensor(res[:, par, :].rearrange("p (r q) -> p r q", r=BR),
                                       Xraw[:, par, 0:H].rearrange("p (q r) -> p r q", r=BR),
                                       bias[:, :].rearrange("p (r q) -> p r q", r=BR), ALU.add)\
                        .then_inc(res_ready, 1)
                else:
                    if isinstance(j, int) and n == STEPS:
                        pool.wait_ge(bias_in, 32)
                    pool.wait_ge(r_loaded[par], 16 * (j - STEPS // 2 + 1))
                    pool.tensor_tensor(res[:, par, :], res[:, par, :], bias[:, :], ALU.add).then_inc(res_ready, 1)

            residual(0, 0, 0)

            def step(j, par, lay, lay1, lay2):
                n = 2 * j + par
                if isinstance(j, int) and n == 0:
                    pool.wait_ge(w_hi, KT)
                    pool.wait_ge(w_lo, KT // 2)
                    pool.memset(craw, 0.0).then_inc(conv_zero, 1)
                if isinstance(j, int) and n in (STEPS - 2, STEPS - 1):
                    pool.wait_ge(x_hi, n + 1)
                    pool.wait_ge(x_lo, n + 1)
                    pool.wait_ge(res_ready, n + 1)
                    v = Xraw[:, par, :].rearrange("p (b q) -> p b q", b=BG)
                    pool.memset(v[:, :, 0:QP:QP - 1], 0.0).then_inc(pad_zero, 1)
                if isinstance(j, int) and n == STEPS - 1:
                    for k in range(1, KT, 2):
                        split_lo(k, 1)
                if lay1 is not None:
                    residual(j + (1 if par else 0), 1 - par, lay1)

            run(pool, step)

        @block.scalar
        def _(act):
            for dst, src in ((emb, embT), (w0s, w0), (w1s, w1), (w2s, w2), (cws, cwT),
                             (b0s, b0.rearrange("(p a) -> p a", a=1)), (b1s, b1.rearrange("(p a) -> p a", a=1)),
                             (b2s[:, 0:E_], b2.partition_broadcast(STEPS)),
                             (cbs, cbias.partition_broadcast(STEPS)), (nbthr, bthr.partition_broadcast(P))):
                act.dma_start(dst, src).then_inc(small_in, 16)
            act.dma_start(mixbs.rearrange("p k o -> p (k o)"), mixb.partition_broadcast(STEPS)).then_inc(mixb_in, 16)
            for a in range(2):
                act.dma_start(mixT[a * C:(a + 1) * C, :, :], mixw).then_inc(mixb_in, 16)

            def split_x(j, par, layer):
                n = 2 * j + par
                if layer == 0:
                    act.wait_ge(x_loaded[par], 16 * (j + 1))
                    w = H
                else:
                    act.wait_ge(g_loaded[par], 16 * BR * (j - STEPS // 2 + 1))
                    w = XW
                if not (isinstance(n, int) and n == 0):
                    act.wait_ge(mixed, 2 * n)
                nc.scalar.copy(Xhi[:, 0:w], Xraw[:, par, 0:w]).then_inc(x_hi, 1)
                if layer == 0:
                    act.wait_ge(agg_ready, n + 1)
                    nc.scalar.copy(Mhi[0:C, 0:C], agg[0:C, :])
                    nc.scalar.copy(Mhi[C:P, C:P], agg[C:P, :]).then_inc(m_hi, 1)

            def split_y(j, par, layer):
                n = 2 * j + par
                if not (isinstance(j, int) and j == 0):
                    act.wait_ge(up_done, n - 1)
                for h in range(2):
                    act.wait_ge(y_half, 2 * n + (h + 1 if layer == 0 else 2))
                    nc.scalar.copy(Yhi[:, par, h * HB:(h + 1) * HB], Y[:, h * HB:(h + 1) * HB])\
                        .then_inc(yhi_half, 1)

            def split_w(k, layer):
                act.wait_ge(w_in[k], 16 * (layer + 1))
                if layer:
                    act.wait_ge(base_tile, k + 1)
                nc.scalar.copy(Whi[:, k, :], stage[:, k, :]).then_inc(w_hi, 1)

            act.wait_ge(mm_cond, 1)
            nc.scalar.activation(h0, psG[:, 0:P], ACT.Gelu, bias=b0s).then_inc(act_cond, 1)
            act.wait_ge(mm_cond, 3)
            nc.scalar.activation(h1, psW[:, 0:P], ACT.Gelu, bias=b1s).then_inc(act_cond, 1)
            act.wait_ge(ag0_in, 16)
            act.wait_ge(consts, 3)
            nc.scalar.copy(AG0hi[:, :, 0:NAG0 - 1], ag0raw).then_inc(s_hi, 1)
            act.wait_ge(dve_cond, 2)
            for a in range(2):
                nc.scalar.activation(ex[:, a, :], lg[:, a, :], ACT.Exp, bias=nmx2[:, a:a + 1],
                                     accum_out=sum2[:, a:a + 1]).then_inc(act_cond, 1)
            for k in range(KT // 2):
                split_w(k, 0)
            split_x(0, 0, 0)
            for k in range(KT // 2, KT - 1):
                split_w(k, 0)
            split_y(0, 0, 0)
            split_w(KT - 1, 0)
            act.wait_ge(b0_in, 16)
            nc.scalar.copy(Bhi[:, 0, :], b0raw).then_inc(s_hi, 1)
            split_x(0, 1, 0)

            def step(j, par, lay, lay1, lay2):
                n = 2 * j + par
                if lay == 0:
                    act.wait_ge(nmax_ready, n + 1)
                    nc.scalar.activation(eg, ag[:, ER:ER + E_], ACT.Exp, bias=nmax, accum_out=den[:, 0:1])
                    nc.scalar.activation(texp, ag[:, ER + E_:ER + E_ + 1], ACT.Exp, bias=nbthr, scale=-1.0)\
                        .then_inc(exp_ready, 1)
                else:
                    act.wait_ge(diff_ready, n - STEPS + 1)
                    nc.scalar.activation(e2, diff, ACT.Exp).then_inc(exp2_ready, 1)
                if lay1 is not None:
                    split_y(j + (1 if par else 0), 1 - par, lay1)
                if lay2 is not None:
                    split_x(j + 1, par, lay2)
                act.wait_ge(tr_done, n + 1)
                nc.scalar.copy(HThi[:, :], psW[:, 0:P]).then_inc(ht_hi, 1)
                if isinstance(j, int) and n == 0:
                    act.wait_ge(l1s_in, 32)
                    nc.scalar.copy(AG1hi[:, :, :], agraw).then_inc(s_hi, 1)
                    nc.scalar.copy(Bhi[:, 1, :], b1raw).then_inc(s_hi, 1)
                    act.wait_ge(conv_in, 16 * 2 * BR)
                    nc.scalar.copy(Chi[:, :, :], craw).then_inc(s_hi, 1)
                if isinstance(j, int) and n == STEPS - 1:
                    for k in range(KT):
                        split_w(k, 1)

            run(act, step)

        @block.vector
        def _(dve):
            def split_x(j, par, layer):
                n = 2 * j + par
                w = H if layer == 0 else XW
                if layer == 0:
                    nc.vector.tensor_tensor(prod[:, :, :], mixT[:, :, :], bcast(attv(n), 2, C), ALU.mult)\
                        .then_inc(prod_ready, 1)
                    dve.wait_ge(prod_ready, n + 1)
                    if not (isinstance(n, int) and n == 0):
                        dve.wait_ge(m_hi, n)
                    nc.vector.tensor_reduce(agg[:, :], prod[:, :, :].rearrange("p k o -> p o k"), AX.X, ALU.add)\
                        .then_inc(agg_ready, 1)
                dve.wait_ge(x_hi, n + 1)
                nc.vector.tensor_tensor(Xlo[:, 0:w], Xraw[:, par, 0:w], as_f32(Xhi[:, 0:w]), ALU.subtract)\
                    .then_inc(x_lo, 1)
                if layer == 0:
                    dve.wait_ge(agg_ready, n + 1)
                    dve.wait_ge(m_hi, n + 1)
                    nc.vector.tensor_tensor(Mlo[0:C, 0:C], agg[0:C, :], as_f32(Mhi[0:C, 0:C]), ALU.subtract)
                    nc.vector.tensor_tensor(Mlo[C:P, C:P], agg[C:P, :], as_f32(Mhi[C:P, C:P]), ALU.subtract)\
                        .then_inc(m_lo, 1)

            def attv(n):
                if isinstance(n, int):
                    return attb[:, n, :]
                return attb[:, bass.ds(n, 1), :].rearrange("p a k -> p (a k)")

            def evacuate_y(j, par, layer):
                n = 2 * j + par
                dve.wait_ge(row_loaded[par], 16 * (j + 1))
                for h in range(2):
                    dve.wait_ge(mixed, 2 * n + h + 1)
                    if not (isinstance(n, int) and n == 0):
                        dve.wait_ge(yhi_half, 2 * n + (h - 1 if layer == 0 else 0))
                    if layer == 0:
                        nc.vector.tensor_tensor(
                            Y[:, h * HB:(h + 1) * HB].rearrange("p (k t) -> p k t", t=P),
                            psT[:, h, :].rearrange("p (k t) -> p k t", t=P),
                            bcast(row[:, par, :], 1, HB // P), ALU.add).then_inc(y_half, 1)
                    else:
                        bg = slice(h * BG // 2, (h + 1) * BG // 2)
                        nc.vector.tensor_tensor(
                            Y[:, :].rearrange("p (t b o) -> p b t o", t=BR, b=BG)[:, bg],
                            psT[:, h, :].rearrange("p (b t o) -> p b t o", b=BG // 2, t=BR),
                            bcast(row[:, par, :].rearrange("p (b o) -> p b o", b=BG)[:, bg], 2, BR), ALU.add)\
                            .then_inc(y_half, 1)

            def split_y(j, par, layer):
                n = 2 * j + par
                for h in range(2):
                    dve.wait_ge(y_half, 2 * n + (h + 1 if layer == 0 else 2))
                    dve.wait_ge(yhi_half, 2 * n + h + 1)
                    nc.vector.tensor_tensor(Ylo[:, par, h * HB:(h + 1) * HB], Y[:, h * HB:(h + 1) * HB],
                                            as_f32(Yhi[:, par, h * HB:(h + 1) * HB]), ALU.subtract)\
                        .then_inc(ylo_half, 1)

            def split_w(k, layer):
                dve.wait_ge(w_hi, KT * layer + k + 1)
                nc.vector.tensor_tensor(Wlo[:, k, :], stage[:, k, :], as_f32(Whi[:, k, :]), ALU.subtract)\
                    .then_inc(w_lo, 1)

            def emit(j, par, layer):
                n = 2 * j + par
                dve.wait_ge(up_done, n + 1)
                dve.wait_ge(res_ready, n + 1)
                if not (isinstance(j, int) and j == 0):
                    dve.wait_ge(stored[par], 16 * j)
                for h in range(2):
                    rr = slice(h * BR // 2, (h + 1) * BR // 2)
                    if layer == 0:
                        to = outb[:, par, :].rearrange("p (r q) -> p r q", r=BR)[:, rr, :]
                    else:
                        to = outb[:, par, :].rearrange("p (q r) -> p r q", r=BR)[:, rr, :]
                    last = nc.vector.tensor_tensor(
                        to, psB[:, 2 * par + h, :].rearrange("p (r q) -> p r q", q=Q),
                        res[:, par, :].rearrange("p (r q) -> p r q", r=BR)[:, rr, :], ALU.add)
                last.then_inc(o_done, 1)

            dve.wait_ge(small_in, 160)
            dve.wait_ge(mm_cond, 4)
            nc.vector.tensor_tensor(lg, psG[0:STEPS, 128:144].rearrange("p (a k) -> p a k", a=2),
                                    bcast(b2s[:, 0:E_], 1, 2), ALU.add).then_inc(dve_cond, 1)
            dve.wait_ge(dve_cond, 1)
            nc.vector.tensor_reduce(nmx2, lg, AX.X, ALU.max, negate=True).then_inc(dve_cond, 1)
            dve.wait_ge(act_cond, 4)
            nc.vector.reciprocal(rec2, sum2).then_inc(dve_cond, 1)
            dve.wait_ge(dve_cond, 3)
            nc.vector.tensor_tensor(att, ex, bcast(rec2, 2, MODES), ALU.mult).then_inc(dve_cond, 1)
            dve.wait_ge(mixb_in, 48)
            dve.wait_ge(dve_cond, 4)
            for a in range(2):
                last = nc.vector.tensor_tensor(aprod[:, a], mixbs, bcast(att[:, a, :], 2, C), ALU.mult)
            last.then_inc(dve_cond, 1)
            dve.wait_ge(dve_cond, 5)
            for a in range(2):
                nc.vector.tensor_reduce(arow[:, a * C:(a + 1) * C], aprod[:, a].rearrange("p k o -> p o k"),
                                        AX.X, ALU.add)
            nc.vector.tensor_tensor(crow.rearrange("p (a o) -> p a o", a=2),
                                    psT[0:STEPS, 0, 0:P].rearrange("p (a o) -> p a o", a=2),
                                    bcast(cbs, 1, 2), ALU.add).then_inc(dve_cond, 1)
            nc.vector.tensor_scalar(nbthr, nbthr, -1.0, None, ALU.mult).then_inc(dve_cond, 1)
            dve.wait_ge(s_hi, 1)
            nc.vector.tensor_tensor(AG0lo[:, :, 0:NAG0 - 1], ag0raw, as_f32(AG0hi[:, :, 0:NAG0 - 1]), ALU.subtract)\
                .then_inc(s_lo, 1)
            for k in range(0, KT // 2, 2):
                split_w(k, 0)
            dve.wait_ge(att_in, 32)
            split_x(0, 0, 0)
            evacuate_y(0, 0, 0)
            split_y(0, 0, 0)
            for k in range(KT // 2, KT, 2):
                split_w(k, 0)
            dve.wait_ge(s_hi, 2)
            nc.vector.tensor_tensor(Blo[:, 0, :], b0raw, as_f32(Bhi[:, 0, :]), ALU.subtract).then_inc(s_lo, 1)
            split_x(0, 1, 0)

            def gates0(j, par):
                n = 2 * j + par
                g = 6 * n
                dve.wait_ge(ag_copied, n + 1)
                nc.vector.tensor_reduce(nmax, ag[:, ER:ER + E_], AX.X, ALU.max, negate=True).then_inc(nmax_ready, 1)
                dve.wait_ge(exp_ready, n + 1)
                nc.vector.tensor_scalar(den[:, 1:2], texp, 1.0, 8.0, ALU.add, ALU.mult).then_inc(gate0, 1)
                dve.wait_ge(gate0, g + 1)
                nc.vector.reciprocal(rec, den).then_inc(gate0, 1)
                dve.wait_ge(gate0, g + 2)
                nc.vector.tensor_scalar(adapted, eg, rec[:, 0:1], rec[:, 1:2], ALU.mult, ALU.subtract)\
                    .then_inc(gate0, 1)
                dve.wait_ge(gate0, g + 3)
                nc.vector.tensor_scalar(wrelu, adapted, 0.0, 0.0, ALU.max, ALU.add, accum_out=wsum).then_inc(gate0, 1)
                dve.wait_ge(gate0, g + 4)
                nc.vector.scalar_tensor_tensor(guard, wsum, 0.0, wsum, ALU.is_equal, ALU.add).then_inc(gate0, 1)
                dve.wait_ge(gate0, g + 5)
                nc.vector.reciprocal(rguard, guard).then_inc(gate0, 1)
                dve.wait_ge(gate0, g + 6)
                return nc.vector.tensor_scalar(wts, wrelu, rguard, 2.0, ALU.mult, ALU.mult)

            def gates1(j, par):
                n = 2 * j + par - STEPS
                g = 5 * n
                nc.vector.max(m8, psG[:, ER:ER + E_]).then_inc(m8_ready, 1)
                dve.wait_ge(m8_ready, n + 1)
                nc.vector.tensor_tensor(diff, m8[:, 1:2], m8[:, 0:1], ALU.subtract).then_inc(diff_ready, 1)
                nc.vector.max_index(idx[:, :], m8, psG[:, ER:ER + E_]).then_inc(ag_copied, 1)
                dve.wait_ge(ag_copied, n + STEPS + 1)
                nc.vector.tensor_copy(idxf, idx[:, 0:2]).then_inc(gate1, 1)
                dve.wait_ge(exp2_ready, n + 1)
                nc.vector.tensor_scalar(s2, e2, 1.0, None, ALU.add).then_inc(gate1, 1)
                dve.wait_ge(gate1, g + 2)
                nc.vector.reciprocal(r2, s2).then_inc(gate1, 1)
                nc.vector.tensor_scalar(hot2, iota[:, :], idxf[:, 1:2], e2, ALU.is_equal, ALU.mult).then_inc(gate1, 1)
                dve.wait_ge(gate1, g + 4)
                nc.vector.scalar_tensor_tensor(hot12, iota[:, :], idxf[:, 0:1], hot2, ALU.is_equal, ALU.add)\
                    .then_inc(gate1, 1)
                dve.wait_ge(gate1, g + 5)
                return nc.vector.tensor_scalar(wts, hot12, r2, 2.0, ALU.mult, ALU.mult)

            def step(j, par, lay, lay1, lay2):
                n = 2 * j + par
                if not (isinstance(n, int) and n == 0):
                    prev = (lay if not isinstance(j, int) else (n - 1) // STEPS)
                    emit(j - (0 if par else 1), 1 - par, prev)
                dve.wait_ge(ag_done, n + 1)
                if lay == 0:
                    nc.vector.tensor_copy(ag[:, 0:NAG0], psG[:, 0:NAG0]).then_inc(ag_copied, 1)
                    gates0(j, par).then_inc(wts_ready, 1)
                else:
                    nc.vector.tensor_copy(ag[:, 0:ER], psG[:, 0:ER])
                    gates1(j, par).then_inc(wts_ready, 1)
                dve.wait_ge(wts_ready, n + 1)
                if not (isinstance(n, int) and n == 0):
                    dve.wait_ge(tr_done, n)
                nc.vector.tensor_tensor(hw[:, :].rearrange("p (e r) -> p e r", e=E_),
                                        ag[:, 0:ER].rearrange("p (e r) -> p e r", e=E_),
                                        bcast(wts, 2, R_), ALU.mult).then_inc(hw_ready, 1)
                if lay1 is not None:
                    evacuate_y(j + (1 if par else 0), 1 - par, lay1)
                    split_y(j + (1 if par else 0), 1 - par, lay1)
                if lay2 is not None:
                    split_x(j + 1, par, lay2)
                dve.wait_ge(ht_hi, n + 1)
                nc.vector.tensor_tensor(HTlo[:, :], psW[:, 0:P], as_f32(HThi[:, :]), ALU.subtract).then_inc(ht_lo, 1)
                if isinstance(j, int) and n == 0:
                    dve.wait_ge(s_hi, 5)
                    nc.vector.tensor_tensor(AG1lo[:, :, :], agraw, as_f32(AG1hi[:, :, :]), ALU.subtract).then_inc(s_lo, 1)
                    nc.vector.tensor_tensor(Blo[:, 1, :], b1raw, as_f32(Bhi[:, 1, :]), ALU.subtract).then_inc(s_lo, 1)
                    nc.vector.tensor_tensor(Clo[:, :, :], craw, as_f32(Chi[:, :, :]), ALU.subtract).then_inc(s_lo, 1)
                if isinstance(j, int) and n == STEPS - 1:
                    for k in range(0, KT, 2):
                        split_w(k, 1)

            run(dve, step)
            emit(STEPS - 1, 1, 1)

        @block.tensor
        def _(pe):
            mm = nc.tensor.matmul

            def mix(j, par, layer):
                n = 2 * j + par
                pe.wait_ge(x_hi, n + 1)
                pe.wait_ge(x_lo, n + 1)
                if layer == 0:
                    pe.wait_ge(m_hi, n + 1)
                    pe.wait_ge(m_lo, n + 1)
                elif isinstance(j, int) and n == STEPS:
                    pe.wait_ge(s_hi, 5)
                    pe.wait_ge(s_lo, 5)
                for h in range(2):
                    if not (isinstance(n, int) and n == 0):
                        pe.wait_ge(y_half, 2 * n - 1 + h)
                    for t in range(4):
                        to = psT[:, h, t * P:(t + 1) * P]
                        k = 4 * h + t
                        if layer == 0:
                            xs = slice(k * P, (k + 1) * P)
                            mm(to, Xhi[:, xs], Mhi[:, :], start=True, stop=False)
                            mm(to, Xhi[:, xs], Mlo[:, :], start=False, stop=False)
                            last = mm(to, Xlo[:, xs], Mhi[:, :], start=False, stop=True)
                        else:
                            b, g = k * QP, k % G
                            cols = ((to, 1, slice(0, P)), (to[:, 0:P // 2], 0, slice(P, P + P // 2)),
                                    (to[:, P // 2:P], 2, slice(P + P // 2, CW)))
                            for s, (dst, d, c) in enumerate(cols):
                                xs = slice(b + d, b + d + Q)
                                mm(dst, Xhi[:, xs], Chi[:, g, c], start=(s == 0), stop=False)
                                mm(dst, Xhi[:, xs], Clo[:, g, c], start=False, stop=False)
                                last = mm(dst, Xlo[:, xs], Chi[:, g, c], start=False, stop=(s == 2))
                    last.then_inc(mixed, 1)

            def agate(j, par, layer):
                n = 2 * j + par
                pe.wait_ge(yhi_half, 2 * n + 2)
                pe.wait_ge(ylo_half, 2 * n + 2)
                if isinstance(n, int) and n == 0:
                    pe.wait_ge(s_hi, 1)
                    pe.wait_ge(s_lo, 1)
                else:
                    pe.wait_ge(ag_copied, n)
                w, hi, lo = (NAG0, AG0hi, AG0lo) if layer == 0 else (NAG1, AG1hi, AG1lo)
                for k in range(KT):
                    yh, yl = Yhi[:, par, k * P:(k + 1) * P], Ylo[:, par, k * P:(k + 1) * P]
                    mm(psG[:, 0:w], yh, hi[:, k, :], start=(k == 0), stop=False)
                    mm(psG[:, 0:w], yh, lo[:, k, :], start=False, stop=False)
                    last = mm(psG[:, 0:w], yl, hi[:, k, :], start=False, stop=(k == KT - 1))
                last.then_inc(ag_done, 1)

            def base(j, par, layer, tiles):
                n = 2 * j + par
                for k in tiles:
                    if k == 0 and not (isinstance(j, int) and j == 0):
                        pe.wait_ge(o_done, n - 1)
                    if isinstance(j, int) and n in (0, STEPS):
                        pe.wait_ge(w_hi, KT * layer + k + 1)
                        if k % 2:
                            pe.wait_ge(w_loP, KT // 2 * layer + k // 2 + 1)
                        else:
                            pe.wait_ge(w_lo, KT // 2 * layer + k // 2 + 1)
                    yh, yl = Yhi[:, par, k * P:(k + 1) * P], Ylo[:, par, k * P:(k + 1) * P]
                    for y, w in ((yh, Whi), (yh, Wlo), (yl, Whi)):
                        for h in range(2):
                            last = mm(psB[:, 2 * par + h, :], y, w[:, k, h * HB:(h + 1) * HB],
                                      start=(k == 0 and y is yh and w is Whi), stop=False)
                    if isinstance(j, int) and n == STEPS - 1:
                        last.then_inc(base_tile, 1)

            def up(j, par, layer):
                n = 2 * j + par
                pe.wait_ge(hw_ready, n + 1)
                if isinstance(n, int) and n == 0:
                    pe.wait_ge(consts, 1)
                    pe.wait_ge(s_hi, 2)
                    pe.wait_ge(s_lo, 2)
                else:
                    pe.wait_ge(ht_lo, n)
                nc.tensor.transpose(psW[:, 0:P], hw[:, :], ident[:, :]).then_inc(tr_done, 1)
                pe.wait_ge(ht_hi, n + 1)
                pe.wait_ge(ht_lo, n + 1)
                for y, w in ((HThi, Bhi), (HThi, Blo), (HTlo, Bhi)):
                    for h in range(2):
                        last = mm(psB[:, 2 * par + h, :], y[:, :], w[:, layer, h * HB:(h + 1) * HB],
                                  start=False, stop=(y is HTlo))
                last.then_inc(up_done, 1)

            pe.wait_ge(small_in, 160)
            mm(psG[:, 0:P], w0s, emb, start=True, stop=True).then_inc(mm_cond, 1)
            for a in range(2):
                last = mm(psT[0:STEPS, 0, a * C:(a + 1) * C], emb[:, a * STEPS:(a + 1) * STEPS], cws,
                          start=True, stop=True)
            last.then_inc(mm_cond, 1)
            pe.wait_ge(act_cond, 1)
            mm(psW[:, 0:P], w1s, h0, start=True, stop=True).then_inc(mm_cond, 1)
            pe.wait_ge(act_cond, 2)
            for a in range(2):
                last = mm(psG[0:STEPS, 128 + a * E_:128 + (a + 1) * E_], h1[:, a * STEPS:(a + 1) * STEPS], w2s,
                          start=True, stop=True)
            last.then_inc(mm_cond, 1)
            pe.wait_ge(dve_cond, 6)
            pe.wait_ge(consts, 3)
            mix(0, 0, 0)

            def step(j, par, lay, lay1, lay2):
                agate(j, par, lay)
                base(j, par, lay, range(0, KT // 2))
                if lay1 is not None:
                    mix(j + (1 if par else 0), 1 - par, lay1)
                base(j, par, lay, range(KT // 2, KT))
                up(j, par, lay)

            run(pe, step)


_OUT = ((128, 64, 1024), "float32")


def kernel(**inputs):
    import numpy as np
    import concourse.bacc as bacc
    from concourse.bass_utils import run_bass_kernel_spmd

    a = {k: np.asarray(v) for k, v in inputs.items()}

    def rq(w):
        return w.reshape(*w.shape[:-1], Q, BR).swapaxes(-1, -2).reshape(w.shape)

    arrays = {
        "x": a["x"].reshape(-1, H),
        "embT": a["cond_128"].reshape(-1, 2, 128).transpose(2, 1, 0).reshape(128, -1),
        "w0": a["L0_cond_W0"], "b0": a["L0_cond_b0"], "w1": a["L0_cond_W1"], "b1": a["L0_cond_b1"],
        "w2": a["L0_cond_W2"], "b2": a["L0_cond_b2"],
        "mixw": a["L0_cond_weight"][..., 0].transpose(2, 0, 1),
        "mixb": a["L0_cond_bias_k"].reshape(-1),
        "l0wT": rq(a["L0_ffn_W_base"].T), "l0b": rq(a["L0_ffn_b_base"]),
        "l0ag": np.concatenate([a["L0_ffn_A"].reshape(ER, H), a["L0_ffn_W_gate"], a["L0_ffn_W_thr"]]).T,
        "bthr": a["L0_ffn_b_thr"],
        "l0B": rq(a["L0_ffn_B"].transpose(0, 2, 1).reshape(ER, H)),
        "convw": a["L1_cond_weight"].reshape(G, GC, GC, TAPS)[..., ::-1].transpose(2, 0, 3, 1),
        "cwT": a["L1_cond_c_weight"].T, "cbias": a["fside_S_0"],
        "l1wT": rq(a["L1_ffn_base_w"].T), "l1b": rq(a["L1_ffn_base_b"]),
        "l1ag": np.concatenate([a["L1_ffn_lora_A"].reshape(ER, H), a["L1_ffn_gate_w"]]).T,
        "l1B": rq(a["L1_ffn_lora_B"].transpose(0, 2, 1).reshape(ER, H)),
    }
    nc = bacc.Bacc("TRN2", target_bir_lowering=False, num_devices=1)
    feeds, args = {}, []
    for name, v in arrays.items():
        v = np.ascontiguousarray(v)
        feeds[f"in_{name}"] = v
        args.append(nc.dram_tensor(f"in_{name}", v.shape, mybir.dt.from_np(v.dtype), kind="ExternalInput").ap())
    out = nc.dram_tensor("out", (a["x"].shape[0] * C, H), F32, kind="ExternalOutput").ap()
    build(nc, *args, out)
    r = run_bass_kernel_spmd(nc, [feeds], core_ids=[0])
    return np.asarray(r.results[0]["out"]).reshape(_OUT[0])
```

```python
import concourse.bass as bass
from concourse import mybir
from contextlib import ExitStack

F32 = mybir.dt.float32
F32R = mybir.dt.float32r
U32 = mybir.dt.uint32
ALU = mybir.AluOpType
ACT = mybir.ActivationFunctionType
AX = mybir.AxisListType

P = 128
C = 64
H = 1024
KT = H // P
HB = 512
E_, R_ = 8, 16
ER = E_ * R_
NAG0 = ER + E_ + 2
NAG1 = ER + E_
G, GC = 4, 16
TAPS, PAD = 9, 4
BR = 8
Q = H // BR
BG = P // GC
QP = Q + 1
XW = BG * QP
MODES = 8
MIX_AFTER = (1, 2, 3, 4)
TURN_AFTER = 5
NC = 4
CH = H // NC


def bcast(ap, axis, n):
    v = ap.unsqueeze(axis)
    shape = list(v.shape)
    shape[axis] = n
    return v.broadcast_to(shape)


def build(nc, x, condw, condr, mixw, l0wT, l0b, l0ag, l0B, convw, l1wT, l1b, l1ag, l1B, out):
    NT = x.shape[0]
    STEPS = NT // P
    x1 = nc.dram_tensor("x1_scratch", [NT, H], F32).ap()
    rows = nc.dram_tensor("row_scratch", [2, STEPS, P], F32).ap()
    atts = nc.dram_tensor("att_scratch", [2, STEPS, MODES], F32).ap()

    with ExitStack() as ctx:
        def sb(name, shape, dt=F32):
            return ctx.enter_context(nc.sbuf_tensor(name, shape, dt))

        def sem(name):
            return ctx.enter_context(nc.semaphore(name))

        stage = sb("stage", [P, KT, H])
        Whi, Wlo = sb("Whi", [P, KT, H], F32R), sb("Wlo", [P, KT, H], F32R)
        AG0 = sb("AG0", [P, KT, 2, NAG0], F32R)
        AG1 = sb("AG1", [P, KT, 2, NAG1], F32R)
        Bhi, Blo = sb("Bhi", [P, 2, H], F32R), sb("Blo", [P, 2, H], F32R)
        CT = sb("CT", [P, G, 2, 2, P], F32R)
        bias = sb("bias", [P, H])
        Xraw = sb("Xraw", [P, 2, XW])
        Xhi, Xlo = sb("Xhi", [P, XW], F32R), sb("Xlo", [P, XW], F32R)
        Y = sb("Y", [P, H])
        Yhi, Ylo = sb("Yhi", [P, 2, H], F32R), sb("Ylo", [P, 2, H], F32R)
        res = sb("res", [P, 2, H])
        outb = sb("outb", [P, 2, H])
        row = sb("row", [P, 2, P])
        attb = sb("attb", [P, STEPS, MODES])
        mixT = sb("mixT", [P, MODES, C])
        prod = sb("prod", [P, MODES, C])
        agg = sb("agg", [P, C])
        M = sb("M", [P, 2, P], F32R)
        ag = sb("ag", [P, NAG0])
        hw = sb("hw", [P, P])
        HThi, HTlo = sb("HThi", [P, P], F32R), sb("HTlo", [P, P], F32R)
        ident = sb("ident", [P, P])
        iota = sb("iota", [P, E_])
        small = sb("small", [P, 64])
        idx = sb("idx", [P, E_], U32)
        nmax, den, rec = small[:, 0:1], small[:, 2:4], small[:, 4:6]
        texp, wsum, guard, rguard = small[:, 6:7], small[:, 7:8], small[:, 8:9], small[:, 9:10]
        nbthr, m8 = small[:, 10:11], small[:, 16:24]
        eg, adapted, wrelu, wts = small[:, 24:32], small[:, 32:40], small[:, 40:48], small[:, 48:56]
        diff, idxf, e2, s2, r2 = small[:, 1:2], small[:, 56:58], small[:, 58:59], small[:, 59:60], small[:, 60:61]
        hot2, hot12 = small[:, 24:32], small[:, 32:40]

        psB = ctx.enter_context(nc.psum_tensor("psB", [P, 4, HB], F32))
        psT = ctx.enter_context(nc.psum_tensor("psT", [P, 2, HB], F32))
        psG = ctx.enter_context(nc.psum_tensor("psG", [P, HB], F32))
        psW = ctx.enter_context(nc.psum_tensor("psW", [P, HB], F32))

        h0, h1 = Y[:, 0:P], Y[:, P:2 * P]
        conds = outb[:, 1, 0:condw.shape[1]]
        w0s, emb, w1s = (conds[:, k * P:(k + 1) * P] for k in range(3))
        w2s, cws = conds[:, 3 * P:3 * P + MODES], conds[:, 3 * P + MODES:3 * P + MODES + C]
        b0s, b1s = conds[:, 456:457], conds[:, 457:458]
        condrs = Y[:, 2 * P:2 * P + condr.shape[0]]
        mixbs = condrs[0:STEPS, 0:MODES * C].rearrange("p (k o) -> p k o", k=MODES)
        b2s, cbs = condrs[0:STEPS, 512:520], condrs[0:STEPS, 520:584]
        bthrs = condrs[:, 584:585]
        lg, ex, att = (Y[0:STEPS, k:k + 16].rearrange("p (a k) -> p a k", a=2) for k in (900, 916, 932))
        nmx2, sum2, rec2 = Y[0:STEPS, 948:950], Y[0:STEPS, 950:952], Y[0:STEPS, 952:954]
        aprod = outb[0:STEPS, 0, :].rearrange("p (a k o) -> p a k o", a=2, k=MODES)
        arow, crow = outb[0:STEPS, 1, 768:896], outb[0:STEPS, 1, 896:1024]
        flat = stage[:, :, :].rearrange("p k n -> p (k n)")
        agraw = flat[:, 0:KT * NAG1].rearrange("p (k n) -> p k n", k=KT)
        b1raw = flat[:, 2048:2048 + H]
        craw = flat[:, 4096:4096 + G * 2 * P].rearrange("p (g w n) -> p g w n", g=G, w=2)
        resflat = res[:, :, :].rearrange("p a n -> p (a n)")
        ag0raw = resflat[:, 0:KT * (NAG0 - 1)].rearrange("p (k n) -> p k n", k=KT)
        b0raw = outb[:, 0, :]

        cond_in, condr_in, mix_in = sem("cond_in"), sem("condr_in"), sem("mix_in")
        ag0_in, b0_in, bias_in = sem("ag0_in"), sem("b0_in"), sem("bias_in")
        w_in = [sem(f"w_in{k}") for k in range(KT)]
        l1s_in, conv_zero, conv_in = sem("l1s_in"), sem("conv_zero"), sem("conv_in")
        ident_zero, consts = sem("ident_zero"), sem("consts")
        mm_cond, act_cond, dve_cond = sem("mm_cond"), sem("act_cond"), sem("dve_cond")
        cond_out, att_in = sem("cond_out"), sem("att_in")
        w_hi, w_lo, w_loP = sem("w_hi"), sem("w_lo"), sem("w_loP")
        s_hi, s_lo, s_loP = sem("s_hi"), sem("s_lo"), sem("s_loP")
        base_tile = sem("base_tile")
        x_loaded = [sem(f"x_loaded{p}") for p in range(2)]
        g_loaded = [sem(f"g_loaded{p}") for p in range(2)]
        r_loaded = [sem(f"r_loaded{p}") for p in range(2)]
        row_loaded = [sem(f"row_loaded{p}") for p in range(2)]
        stored = [sem(f"stored{p}") for p in range(2)]
        pad_zero = sem("pad_zero")
        x_hi, x_lo = sem("x_hi"), sem("x_lo")
        prod_ready, agg_ready, m_hi, m_lo = sem("prod_ready"), sem("agg_ready"), sem("m_hi"), sem("m_lo")
        mixed, y_part, y_chunk, yhi_half, ylo_half = sem("mixed"), sem("y_part"), sem("y_chunk"), sem("yhi_half"), sem("ylo_half")
        ag_done, ag_part, ag_gate, ag_copied = sem("ag_done"), sem("ag_part"), sem("ag_gate"), sem("ag_copied")
        nmax_ready, exp_ready, gate0 = sem("nmax_ready"), sem("exp_ready"), sem("gate0")
        m8_ready, diff_ready, exp2_ready, gate1 = sem("m8_ready"), sem("diff_ready"), sem("exp2_ready"), sem("gate1")
        hw_ready, tr_done, ht_hi, ht_lo = sem("hw_ready"), sem("tr_done"), sem("ht_hi"), sem("ht_lo")
        wts_ready, up_done = sem("wts_ready"), sem("up_done")
        res_ready, o_done = sem("res_ready"), sem("o_done")

        def as_f32(ap):
            return ap.bitcast(F32)

        def run(eng, step):
            def layer(n):
                return n // STEPS if n < 2 * STEPS else None

            def peeled(n):
                step(n // 2, n % 2, layer(n), layer(n + 1), layer(n + 2))

            for lay in range(2):
                first = lay * STEPS
                peeled(first)
                peeled(first + 1)
                with eng.Fori(first // 2 + 1, (first + STEPS) // 2 - 1) as j:
                    step(j, 0, lay, lay, lay)
                    step(j, 1, lay, lay, lay)
                peeled(first + STEPS - 2)
                peeled(first + STEPS - 1)

        block = ctx.enter_context(nc.Block())

        @block.sync
        def _(sp):
            def load_x(j, par, layer):
                n = 2 * j + par
                if layer == 0:
                    sp.dma_start(Xraw[:, par, 0:H], x[bass.ds(n * P, P), :]).then_inc(x_loaded[par], 16)
                else:
                    dst = Xraw[:, par, :].rearrange("p (b q) -> p b q", b=BG)
                    m = n - STEPS
                    src = x1[bass.ds(m * P, P), :].rearrange("(b i) (r q) -> r i b q", b=BG, r=BR)
                    for r in range(BR):
                        first = 1 if r < PAD else 0
                        sp.dma_start(dst[r * GC:(r + 1) * GC, :, first:first + Q], src[(r + PAD) % BR])\
                            .then_inc(g_loaded[par], 16)
                sp.dma_start(row[:, par, :], rows[layer, bass.ds(n - layer * STEPS, 1), :].rearrange("a t -> (a t)")
                             .partition_broadcast(P)).then_inc(row_loaded[par], 16)

            sp.dma_start(conds, condw).then_inc(cond_in, 16)
            sp.dma_start(Xraw[:, 0, 0:H], x[0:P, :]).then_inc(x_loaded[0], 16)
            sp.dma_start(ag0raw, l0ag.rearrange("(k p) n -> p k n", p=P)).then_inc(ag0_in, 16)

            def load_w(ks):
                for k in ks:
                    sp.dma_start(stage[:, k, :], l0wT[k * P:(k + 1) * P, :]).then_inc(w_in[k], 16)

            load_w(range(0, 1))
            sp.wait_ge(dve_cond, 4)
            sp.dma_start(atts.rearrange("a s k -> s a k"), att).then_inc(cond_out, 16)
            load_w(range(1, 3))
            sp.wait_ge(cond_out, 16)
            for a in range(2):
                sp.dma_start(attb[a * C:(a + 1) * C, :, :].rearrange("p s k -> p (s k)"),
                             atts[a].rearrange("s k -> (s k)").partition_broadcast(C)).then_inc(att_in, 16)
            load_w(range(3, 4))
            sp.wait_ge(dve_cond, 6)
            sp.dma_start(rows[0], arow).then_inc(cond_out, 16)
            sp.dma_start(rows[1], crow).then_inc(cond_out, 16)
            load_w(range(4, 6))
            sp.wait_ge(cond_out, 48)
            for par in range(2):
                sp.dma_start(row[:, par, :], rows[0, par, :].partition_broadcast(P)).then_inc(row_loaded[par], 16)
            load_w(range(6, KT))
            sp.dma_start(Xraw[:, 1, 0:H], x[P:2 * P, :]).then_inc(x_loaded[1], 16)
            sp.dma_start(b0raw, l0B).then_inc(b0_in, 16)
            sp.dma_start(bias[:, :], l0b.partition_broadcast(P)).then_inc(bias_in, 16)

            def step(j, par, lay, lay1, lay2):
                n = 2 * j + par
                if lay2 is not None:
                    sp.wait_ge(x_hi, n + 1)
                    sp.wait_ge(x_lo, n + 1)
                    if lay == 0:
                        sp.wait_ge(res_ready, n + 1)
                    sp.wait_ge(y_chunk, NC * n + NC)
                    if lay2 == 1:
                        if lay == 0:
                            sp.wait_ge(pad_zero, par + 1)
                        sp.wait_ge(stored[par], 16 * (j - STEPS // 2 + 2))
                    load_x(j + 1, par, lay2)
                if lay == 0 and isinstance(j, int) and n == 0:
                    sp.wait_ge(w_hi, KT)
                    sp.wait_ge(w_lo, KT // 2)
                    sp.wait_ge(w_loP, KT // 2)
                    sp.dma_start(agraw, l1ag.rearrange("(p k) n -> p k n", p=P)).then_inc(l1s_in, 16)
                    sp.dma_start(b1raw, l1B).then_inc(l1s_in, 16)
                    sp.wait_ge(conv_zero, 1)
                    for r in range(BR):
                        to = craw[r * GC:(r + 1) * GC, :, :, :].rearrange("p g w (t o) -> p g w t o", o=GC)
                        sp.dma_start(to[:, :, 0, 0:r + 1, :], convw[:, :, BR - r:BR + 1, :]).then_inc(conv_in, 16)
                        sp.dma_start(to[:, :, 1, r:BR, :], convw[:, :, 0:BR - r, :]).then_inc(conv_in, 16)
                if lay == 0 and isinstance(j, int) and n == 1:
                    sp.wait_ge(s_hi, 5)
                    sp.wait_ge(s_loP, 3)
                    for k in range(KT):
                        sp.dma_start(stage[:, k, :], l1wT.rearrange("(p k) n -> p k n", p=P)[:, k, :])\
                            .then_inc(w_in[k], 16)
                if isinstance(j, int) and n == STEPS - 1:
                    sp.dma_start(bias[:, :], l1b.partition_broadcast(P)).then_inc(bias_in, 16)
                sp.wait_ge(o_done, n + 1)
                to = x1 if lay == 0 else out
                sp.dma_start(to[bass.ds((n - lay * STEPS) * P, P), :], outb[:, par, :]).then_inc(stored[par], 16)
                if lay2 == 1:
                    sp.dma_start(res[:, par, :], x1[bass.ds((n + 2 - STEPS) * P, P), :]).then_inc(r_loaded[par], 16)

            run(sp, step)
            for par in range(2):
                sp.wait_ge(stored[par], 16 * STEPS)

        @block.gpsimd
        def _(pool):
            pool.memset(ident[:, :], 0.0).then_inc(ident_zero, 1)
            pool.wait_ge(ident_zero, 1)
            pool.affine_select(out=ident[:, :], in_=ident[:, :], compare_op=ALU.not_equal, fill=1.0, base=0,
                               pattern=[[-1, P]], channel_multiplier=1).then_inc(consts, 1)
            for e in range(E_):
                last = pool.memset(iota[:, e:e + 1], float(e))
            last.then_inc(consts, 1)
            pool.memset(as_f32(M[:, :, :]), 0.0)
            pool.memset(as_f32(AG0[:, :, :, :])[:, :, :, NAG0 - 1:NAG0], 0.0).then_inc(consts, 1)

            def split_lo(k, layer):
                pool.wait_ge(w_hi, KT * layer + k + 1)
                pool.tensor_tensor(Wlo[:, k, :], stage[:, k, :], as_f32(Whi[:, k, :]), ALU.subtract)\
                    .then_inc(w_loP, 1)

            for k in range(1, KT, 2):
                split_lo(k, 0)
            pool.wait_ge(bias_in, 16)
            pool.wait_ge(s_lo, 1)

            def residual(j, par, layer):
                n = 2 * j + par
                if layer == 0:
                    pool.wait_ge(x_loaded[par], 16 * (j + 1))
                    if not (isinstance(j, int) and j == 0):
                        pool.wait_ge(o_done, n - 1)
                    pool.tensor_tensor(res[:, par, :].rearrange("p (r q) -> p r q", r=BR),
                                       Xraw[:, par, 0:H].rearrange("p (q r) -> p r q", r=BR),
                                       bias[:, :].rearrange("p (r q) -> p r q", r=BR), ALU.add)\
                        .then_inc(res_ready, 1)
                else:
                    if isinstance(j, int) and n == STEPS:
                        pool.wait_ge(bias_in, 32)
                    pool.wait_ge(r_loaded[par], 16 * (j - STEPS // 2 + 1))
                    pool.tensor_tensor(res[:, par, :], res[:, par, :], bias[:, :], ALU.add).then_inc(res_ready, 1)

            residual(0, 0, 0)

            def step(j, par, lay, lay1, lay2):
                n = 2 * j + par
                if isinstance(j, int) and n == 0:
                    pool.wait_ge(w_hi, KT)
                    pool.wait_ge(w_lo, KT // 2)
                    pool.memset(craw, 0.0).then_inc(conv_zero, 1)
                    residual(0, 1, 0)
                    for k, (lo, raw, hi) in enumerate((
                            (AG1[:, :, 1, :], agraw, AG1[:, :, 0, :]), (Blo[:, 1, :], b1raw, Bhi[:, 1, :]),
                            (CT[:, :, :, 1, :], craw, CT[:, :, :, 0, :]))):
                        pool.wait_ge(s_hi, 3 + k)
                        pool.tensor_tensor(lo, raw, as_f32(hi), ALU.subtract).then_inc(s_loP, 1)
                    return
                if isinstance(j, int) and n in (STEPS - 2, STEPS - 1):
                    pool.wait_ge(x_hi, n + 1)
                    pool.wait_ge(x_lo, n + 1)
                    pool.wait_ge(res_ready, n + 1)
                    v = Xraw[:, par, :].rearrange("p (b q) -> p b q", b=BG)
                    pool.memset(v[:, :, 0:QP:Q], 0.0).then_inc(pad_zero, 1)
                if isinstance(j, int) and n == STEPS - 1:
                    for k in range(1, KT, 2):
                        split_lo(k, 1)
                if lay1 is not None:
                    residual(j + (1 if par else 0), 1 - par, lay1)

            run(pool, step)

        @block.scalar
        def _(act):
            act.dma_start(condrs, condr.partition_broadcast(P)).then_inc(condr_in, 16)
            for a in range(2):
                act.dma_start(mixT[a * C:(a + 1) * C, :, :], mixw).then_inc(mix_in, 16)

            def high_x(j, par, layer):
                n = 2 * j + par
                if layer == 0:
                    act.wait_ge(x_loaded[par], 16 * (j + 1))
                    w = H
                else:
                    act.wait_ge(g_loaded[par], 16 * BR * (j - STEPS // 2 + 1))
                    w = XW
                if not (isinstance(n, int) and n == 0):
                    act.wait_ge(mixed, NC * n)
                nc.scalar.copy(Xhi[:, 0:w], Xraw[:, par, 0:w]).then_inc(x_hi, 1)

            def high_m(n):
                act.wait_ge(agg_ready, n + 1)
                nc.scalar.copy(M[0:C, 0, 0:C], agg[0:C, :])
                nc.scalar.copy(M[C:P, 0, C:P], agg[C:P, :]).then_inc(m_hi, 1)

            def split_y(j, par, layer):
                n = 2 * j + par
                if not (isinstance(j, int) and j == 0):
                    act.wait_ge(up_done, n - 1)
                for h in range(2):
                    act.wait_ge(y_chunk, NC * n + (2 * h + 2 if layer == 0 else NC))
                    nc.scalar.copy(Yhi[:, par, h * HB:(h + 1) * HB], Y[:, h * HB:(h + 1) * HB])\
                        .then_inc(yhi_half, 1)

            def split_w(k, layer):
                act.wait_ge(w_in[k], 16 * (layer + 1))
                if layer:
                    act.wait_ge(base_tile, k + 1)
                nc.scalar.copy(Whi[:, k, :], stage[:, k, :]).then_inc(w_hi, 1)

            act.wait_ge(mm_cond, 1)
            nc.scalar.activation(h0, psG[:, 0:P], ACT.Gelu, bias=b0s).then_inc(act_cond, 1)
            act.wait_ge(mm_cond, 3)
            nc.scalar.activation(h1, psW[:, 0:P], ACT.Gelu, bias=b1s).then_inc(act_cond, 1)
            high_x(0, 0, 0)
            act.wait_ge(dve_cond, 2)
            for a in range(2):
                nc.scalar.activation(ex[:, a, :], lg[:, a, :], ACT.Exp, bias=nmx2[:, a:a + 1],
                                     accum_out=sum2[:, a:a + 1]).then_inc(act_cond, 1)
            act.wait_ge(ag0_in, 16)
            act.wait_ge(consts, 3)
            nc.scalar.copy(AG0[:, :, 0, 0:NAG0 - 1], ag0raw).then_inc(s_hi, 1)
            for k in range(2):
                split_w(k, 0)
            high_m(0)
            for k in range(2, KT // 2):
                split_w(k, 0)
            split_y(0, 0, 0)
            for k in range(KT // 2, KT):
                split_w(k, 0)
            high_x(0, 1, 0)
            high_m(1)
            act.wait_ge(b0_in, 16)
            nc.scalar.copy(Bhi[:, 0, :], b0raw).then_inc(s_hi, 1)

            def step(j, par, lay, lay1, lay2):
                n = 2 * j + par
                if lay == 0:
                    act.wait_ge(nmax_ready, n + 1)
                    nc.scalar.activation(eg, ag[:, ER:ER + E_], ACT.Exp, bias=nmax, accum_out=den[:, 0:1])
                    nc.scalar.activation(texp, ag[:, ER + E_:ER + E_ + 1], ACT.Exp, bias=nbthr, scale=-1.0)\
                        .then_inc(exp_ready, 1)
                else:
                    act.wait_ge(diff_ready, n - STEPS + 1)
                    nc.scalar.activation(e2, diff, ACT.Exp).then_inc(exp2_ready, 1)
                if lay1 is not None:
                    split_y(j + (1 if par else 0), 1 - par, lay1)
                act.wait_ge(tr_done, n + 1)
                nc.scalar.copy(HThi[:, :], psW[:, 0:P]).then_inc(ht_hi, 1)
                if lay2 is not None:
                    high_x(j + 1, par, lay2)
                    if lay2 == 0:
                        high_m(n + 2)
                if isinstance(j, int) and n == 0:
                    act.wait_ge(l1s_in, 32)
                    nc.scalar.copy(AG1[:, :, 0, :], agraw).then_inc(s_hi, 1)
                    nc.scalar.copy(Bhi[:, 1, :], b1raw).then_inc(s_hi, 1)
                    act.wait_ge(conv_in, 16 * 2 * BR)
                    nc.scalar.copy(CT[:, :, :, 0, :], craw).then_inc(s_hi, 1)
                if isinstance(j, int) and n == STEPS - 1:
                    for k in range(KT):
                        split_w(k, 1)

            run(act, step)

        @block.vector
        def _(dve):
            def mixing_matrix(n):
                nc.vector.tensor_tensor(prod[:, :, :], mixT[:, :, :], bcast(attv(n), 2, C), ALU.mult)\
                    .then_inc(prod_ready, 1)
                dve.wait_ge(prod_ready, n + 1)
                if not (isinstance(n, int) and n == 0):
                    dve.wait_ge(m_hi, n)
                nc.vector.tensor_reduce(agg[:, :], prod[:, :, :].rearrange("p k o -> p o k"), AX.X, ALU.add)\
                    .then_inc(agg_ready, 1)

            def low_x(j, par, layer):
                n = 2 * j + par
                w = H if layer == 0 else XW
                dve.wait_ge(x_hi, n + 1)
                nc.vector.tensor_tensor(Xlo[:, 0:w], Xraw[:, par, 0:w], as_f32(Xhi[:, 0:w]), ALU.subtract)\
                    .then_inc(x_lo, 1)

            def low_m(n):
                dve.wait_ge(agg_ready, n + 1)
                dve.wait_ge(m_hi, n + 1)
                nc.vector.tensor_tensor(M[0:C, 1, 0:C], agg[0:C, :], as_f32(M[0:C, 0, 0:C]), ALU.subtract)
                nc.vector.tensor_tensor(M[C:P, 1, C:P], agg[C:P, :], as_f32(M[C:P, 0, C:P]), ALU.subtract)\
                    .then_inc(m_lo, 1)

            def attv(n):
                if isinstance(n, int):
                    return attb[:, n, :]
                return attb[:, bass.ds(n, 1), :].rearrange("p a k -> p (a k)")

            def evacuate_y(j, par, layer):
                n = 2 * j + par
                dve.wait_ge(row_loaded[par], 16 * (j + 1))
                for c in range(NC):
                    h = c // 2
                    dve.wait_ge(mixed, NC * n + c + 1)
                    if not (isinstance(n, int) and n == 0):
                        dve.wait_ge(yhi_half, 2 * n + (h - 1 if layer == 0 else 0))
                    bank = psT[:, c % 2, :].rearrange("p (b s n) -> p b s n", b=2, s=2)
                    if layer == 0:
                        y = Y[:, c * CH:(c + 1) * CH].rearrange("p (b n) -> p b n", b=2)
                        add = bcast(row[:, par, :], 1, 2)
                        parts = (bank[:, :, 0, :], bank[:, :, 1, :])
                    else:
                        y = Y[:, :].rearrange("p (t b o) -> p b t o", t=BR, b=BG)[:, 2 * c:2 * c + 2]
                        add = bcast(row[:, par, c * 2 * GC:(c + 1) * 2 * GC].rearrange("p (b o) -> p b o", b=2), 2, BR)
                        parts = tuple(bank[:, :, s, :].rearrange("p b (t o) -> p b t o", t=BR) for s in range(2))
                    nc.vector.tensor_tensor(y, parts[0], add, ALU.add).then_inc(y_part, 1)
                    dve.wait_ge(y_part, NC * n + c + 1)
                    nc.vector.tensor_tensor(y, parts[1], y, ALU.add).then_inc(y_chunk, 1)

            def split_y(j, par, layer):
                n = 2 * j + par
                for h in range(2):
                    dve.wait_ge(y_chunk, NC * n + (2 * h + 2 if layer == 0 else NC))
                    dve.wait_ge(yhi_half, 2 * n + h + 1)
                    nc.vector.tensor_tensor(Ylo[:, par, h * HB:(h + 1) * HB], Y[:, h * HB:(h + 1) * HB],
                                            as_f32(Yhi[:, par, h * HB:(h + 1) * HB]), ALU.subtract)\
                        .then_inc(ylo_half, 1)

            def split_w(k, layer):
                dve.wait_ge(w_hi, KT * layer + k + 1)
                nc.vector.tensor_tensor(Wlo[:, k, :], stage[:, k, :], as_f32(Whi[:, k, :]), ALU.subtract)\
                    .then_inc(w_lo, 1)

            def emit(j, par, layer):
                n = 2 * j + par
                dve.wait_ge(up_done, n + 1)
                dve.wait_ge(res_ready, n + 1)
                if not (isinstance(j, int) and j == 0):
                    dve.wait_ge(stored[par], 16 * j)
                for h in range(2):
                    rr = slice(h * BR // 2, (h + 1) * BR // 2)
                    if layer == 0:
                        to = outb[:, par, :].rearrange("p (r q) -> p r q", r=BR)[:, rr, :]
                    else:
                        to = outb[:, par, :].rearrange("p (q r) -> p r q", r=BR)[:, rr, :]
                    last = nc.vector.tensor_tensor(
                        to, psB[:, 2 * par + h, :].rearrange("p (r q) -> p r q", q=Q),
                        res[:, par, :].rearrange("p (r q) -> p r q", r=BR)[:, rr, :], ALU.add)
                last.then_inc(o_done, 1)

            dve.wait_ge(condr_in, 16)
            dve.wait_ge(mm_cond, 4)
            nc.vector.tensor_tensor(lg, psG[0:STEPS, 128:144].rearrange("p (a k) -> p a k", a=2),
                                    bcast(b2s[:, 0:E_], 1, 2), ALU.add).then_inc(dve_cond, 1)
            dve.wait_ge(dve_cond, 1)
            nc.vector.tensor_reduce(nmx2, lg, AX.X, ALU.max, negate=True).then_inc(dve_cond, 1)
            dve.wait_ge(act_cond, 4)
            nc.vector.reciprocal(rec2, sum2).then_inc(dve_cond, 1)
            dve.wait_ge(dve_cond, 3)
            nc.vector.tensor_tensor(att, ex, bcast(rec2, 2, MODES), ALU.mult).then_inc(dve_cond, 1)
            low_x(0, 0, 0)
            dve.wait_ge(dve_cond, 4)
            for a in range(2):
                last = nc.vector.tensor_tensor(aprod[:, a], mixbs, bcast(att[:, a, :], 2, C), ALU.mult)
            last.then_inc(dve_cond, 1)
            dve.wait_ge(dve_cond, 5)
            for a in range(2):
                nc.vector.tensor_reduce(arow[:, a * C:(a + 1) * C], aprod[:, a].rearrange("p k o -> p o k"),
                                        AX.X, ALU.add)
            nc.vector.tensor_tensor(crow.rearrange("p (a o) -> p a o", a=2),
                                    psT[0:STEPS, 0, 0:P].rearrange("p (a o) -> p a o", a=2),
                                    bcast(cbs, 1, 2), ALU.add).then_inc(dve_cond, 1)
            nc.vector.tensor_scalar(nbthr, bthrs, -1.0, None, ALU.mult).then_inc(dve_cond, 1)
            dve.wait_ge(s_hi, 1)
            nc.vector.tensor_tensor(AG0[:, :, 1, 0:NAG0 - 1], ag0raw, as_f32(AG0[:, :, 0, 0:NAG0 - 1]), ALU.subtract)\
                .then_inc(s_lo, 1)
            dve.wait_ge(att_in, 32)
            dve.wait_ge(mix_in, 32)
            mixing_matrix(0)
            split_w(0, 0)
            low_m(0)
            split_w(2, 0)
            evacuate_y(0, 0, 0)
            split_y(0, 0, 0)
            for k in range(KT // 2, KT, 2):
                split_w(k, 0)
            mixing_matrix(1)
            low_x(0, 1, 0)
            low_m(1)
            dve.wait_ge(s_hi, 2)
            nc.vector.tensor_tensor(Blo[:, 0, :], b0raw, as_f32(Bhi[:, 0, :]), ALU.subtract).then_inc(s_lo, 1)

            def gates0(j, par):
                n = 2 * j + par
                g = 6 * n
                nc.vector.tensor_reduce(nmax, ag[:, ER:ER + E_], AX.X, ALU.max, negate=True).then_inc(nmax_ready, 1)
                dve.wait_ge(exp_ready, n + 1)
                nc.vector.tensor_scalar(den[:, 1:2], texp, 1.0, 8.0, ALU.add, ALU.mult).then_inc(gate0, 1)
                dve.wait_ge(gate0, g + 1)
                nc.vector.reciprocal(rec, den).then_inc(gate0, 1)
                dve.wait_ge(gate0, g + 2)
                nc.vector.tensor_scalar(adapted, eg, rec[:, 0:1], rec[:, 1:2], ALU.mult, ALU.subtract)\
                    .then_inc(gate0, 1)
                dve.wait_ge(gate0, g + 3)
                nc.vector.tensor_scalar(wrelu, adapted, 0.0, 0.0, ALU.max, ALU.add, accum_out=wsum).then_inc(gate0, 1)
                dve.wait_ge(gate0, g + 4)
                nc.vector.scalar_tensor_tensor(guard, wsum, 0.0, wsum, ALU.is_equal, ALU.add).then_inc(gate0, 1)
                dve.wait_ge(gate0, g + 5)
                nc.vector.reciprocal(rguard, guard).then_inc(gate0, 1)
                dve.wait_ge(gate0, g + 6)
                return nc.vector.tensor_scalar(wts, wrelu, rguard, 2.0, ALU.mult, ALU.mult)

            def gates1(j, par):
                n = 2 * j + par - STEPS
                g = 6 * n
                nc.vector.max(m8, ag[:, ER:ER + E_]).then_inc(m8_ready, 1)
                dve.wait_ge(m8_ready, n + 1)
                nc.vector.tensor_tensor(diff, m8[:, 1:2], m8[:, 0:1], ALU.subtract).then_inc(diff_ready, 1)
                nc.vector.max_index(idx[:, :], m8, ag[:, ER:ER + E_]).then_inc(gate1, 1)
                dve.wait_ge(gate1, g + 1)
                nc.vector.tensor_copy(idxf, idx[:, 0:2]).then_inc(gate1, 1)
                dve.wait_ge(exp2_ready, n + 1)
                nc.vector.tensor_scalar(s2, e2, 1.0, None, ALU.add).then_inc(gate1, 1)
                dve.wait_ge(gate1, g + 3)
                nc.vector.reciprocal(r2, s2).then_inc(gate1, 1)
                nc.vector.tensor_scalar(hot2, iota[:, :], idxf[:, 1:2], e2, ALU.is_equal, ALU.mult).then_inc(gate1, 1)
                dve.wait_ge(gate1, g + 5)
                nc.vector.scalar_tensor_tensor(hot12, iota[:, :], idxf[:, 0:1], hot2, ALU.is_equal, ALU.add)\
                    .then_inc(gate1, 1)
                dve.wait_ge(gate1, g + 6)
                return nc.vector.tensor_scalar(wts, hot12, r2, 2.0, ALU.mult, ALU.mult)

            def step(j, par, lay, lay1, lay2):
                n = 2 * j + par
                if not (isinstance(n, int) and n == 0):
                    prev = (lay if not isinstance(j, int) else (n - 1) // STEPS)
                    emit(j - (0 if par else 1), 1 - par, prev)
                dve.wait_ge(ag_done, n + 1)
                w = NAG0 if lay == 0 else NAG1
                nc.vector.tensor_copy(ag[:, 0:w], psG[:, 0:w]).then_inc(ag_part, 1)
                dve.wait_ge(ag_part, n + 1)
                nc.vector.tensor_tensor(ag[:, ER:w], psG[:, w + ER:2 * w], ag[:, ER:w], ALU.add).then_inc(ag_gate, 1)
                dve.wait_ge(ag_gate, n + 1)
                nc.vector.tensor_tensor(ag[:, 0:ER], psG[:, w:w + ER], ag[:, 0:ER], ALU.add).then_inc(ag_copied, 1)
                (gates0 if lay == 0 else gates1)(j, par).then_inc(wts_ready, 1)
                dve.wait_ge(wts_ready, n + 1)
                dve.wait_ge(ag_copied, n + 1)
                if not (isinstance(n, int) and n == 0):
                    dve.wait_ge(tr_done, n)
                nc.vector.tensor_tensor(hw[:, :].rearrange("p (e r) -> p e r", e=E_),
                                        ag[:, 0:ER].rearrange("p (e r) -> p e r", e=E_),
                                        bcast(wts, 2, R_), ALU.mult).then_inc(hw_ready, 1)
                if lay1 is not None:
                    evacuate_y(j + (1 if par else 0), 1 - par, lay1)
                    split_y(j + (1 if par else 0), 1 - par, lay1)
                dve.wait_ge(ht_hi, n + 1)
                nc.vector.tensor_tensor(HTlo[:, :], psW[:, 0:P], as_f32(HThi[:, :]), ALU.subtract).then_inc(ht_lo, 1)
                if lay2 is not None:
                    if lay2 == 0:
                        mixing_matrix(n + 2)
                    low_x(j + 1, par, lay2)
                    if lay2 == 0:
                        low_m(n + 2)
                if isinstance(j, int) and n == STEPS - 1:
                    for k in range(0, KT, 2):
                        split_w(k, 1)

            run(dve, step)
            emit(STEPS - 1, 1, 1)

        @block.tensor
        def _(pe):
            mm = nc.tensor.matmul

            def mix(j, par, layer, c):
                n = 2 * j + par
                if c == 0:
                    pe.wait_ge(x_hi, n + 1)
                    pe.wait_ge(x_lo, n + 1)
                    if layer == 0:
                        pe.wait_ge(m_hi, n + 1)
                        pe.wait_ge(m_lo, n + 1)
                    elif isinstance(j, int) and n == STEPS:
                        pe.wait_ge(s_hi, 5)
                        pe.wait_ge(s_loP, 3)
                if not (isinstance(n, int) and n == 0 and c < 2):
                    pe.wait_ge(y_chunk, NC * n + c - 1)
                for t in range(2):
                    to = psT[:, c % 2, t * 2 * P:(t + 1) * 2 * P]
                    k = 2 * c + t
                    if layer == 0:
                        xs = slice(k * P, (k + 1) * P)
                        mm(to, Xhi[:, xs], M[:, :, :].rearrange("p s n -> p (s n)"), start=True, stop=False)
                        last = mm(to[:, 0:P], Xlo[:, xs], M[:, 0, :], start=False, stop=True)
                    else:
                        g = k % G
                        for w in range(2):
                            xs = slice(k * QP + w, k * QP + w + Q)
                            mm(to, Xhi[:, xs], CT[:, g, w, :, :].rearrange("p s n -> p (s n)"),
                               start=(w == 0), stop=False)
                            last = mm(to[:, 0:P], Xlo[:, xs], CT[:, g, w, 0, :], start=False, stop=(w == 1))
                last.then_inc(mixed, 1)

            def agate(j, par, layer):
                n = 2 * j + par
                pe.wait_ge(yhi_half, 2 * n + 2)
                pe.wait_ge(ylo_half, 2 * n + 2)
                if isinstance(n, int) and n == 0:
                    pe.wait_ge(s_hi, 1)
                    pe.wait_ge(s_lo, 1)
                else:
                    pe.wait_ge(ag_copied, n)
                w, agw = (NAG0, AG0) if layer == 0 else (NAG1, AG1)
                for k in range(KT):
                    yh, yl = Yhi[:, par, k * P:(k + 1) * P], Ylo[:, par, k * P:(k + 1) * P]
                    mm(psG[:, 0:2 * w], yh, agw[:, k, :, :].rearrange("p s n -> p (s n)"), start=(k == 0), stop=False)
                    last = mm(psG[:, 0:w], yl, agw[:, k, 0, :], start=False, stop=(k == KT - 1))
                last.then_inc(ag_done, 1)

            def base(j, par, layer, tiles):
                n = 2 * j + par
                for k in tiles:
                    if k == 0 and not (isinstance(j, int) and j == 0):
                        pe.wait_ge(o_done, n - 1)
                    if isinstance(j, int) and n in (0, STEPS):
                        pe.wait_ge(w_hi, KT * layer + k + 1)
                        if k % 2:
                            pe.wait_ge(w_loP, KT // 2 * layer + k // 2 + 1)
                        else:
                            pe.wait_ge(w_lo, KT // 2 * layer + k // 2 + 1)
                    yh, yl = Yhi[:, par, k * P:(k + 1) * P], Ylo[:, par, k * P:(k + 1) * P]
                    for y, w in ((yh, Whi), (yh, Wlo), (yl, Whi)):
                        for h in range(2):
                            last = mm(psB[:, 2 * par + h, :], y, w[:, k, h * HB:(h + 1) * HB],
                                      start=(k == 0 and y is yh and w is Whi), stop=False)
                    if isinstance(j, int) and n == STEPS - 1:
                        last.then_inc(base_tile, 1)

            def turn(j, par):
                n = 2 * j + par
                pe.wait_ge(hw_ready, n + 1)
                if isinstance(n, int) and n == 0:
                    pe.wait_ge(consts, 1)
                else:
                    pe.wait_ge(ht_lo, n)
                nc.tensor.transpose(psW[:, 0:P], hw[:, :], ident[:, :]).then_inc(tr_done, 1)

            def up(j, par, layer):
                n = 2 * j + par
                if isinstance(n, int) and n == 0:
                    pe.wait_ge(s_hi, 2)
                    pe.wait_ge(s_lo, 2)
                pe.wait_ge(ht_hi, n + 1)
                pe.wait_ge(ht_lo, n + 1)
                for y, w in ((HThi, Bhi), (HThi, Blo), (HTlo, Bhi)):
                    for h in range(2):
                        last = mm(psB[:, 2 * par + h, :], y[:, :], w[:, layer, h * HB:(h + 1) * HB],
                                  start=False, stop=(y is HTlo))
                last.then_inc(up_done, 1)

            pe.wait_ge(cond_in, 16)
            mm(psG[:, 0:P], w0s, emb, start=True, stop=True).then_inc(mm_cond, 1)
            for a in range(2):
                last = mm(psT[0:STEPS, 0, a * C:(a + 1) * C], emb[:, a * STEPS:(a + 1) * STEPS], cws,
                          start=True, stop=True)
            last.then_inc(mm_cond, 1)
            pe.wait_ge(act_cond, 1)
            mm(psW[:, 0:P], w1s, h0, start=True, stop=True).then_inc(mm_cond, 1)
            pe.wait_ge(act_cond, 2)
            for a in range(2):
                last = mm(psG[0:STEPS, 128 + a * E_:128 + (a + 1) * E_], h1[:, a * STEPS:(a + 1) * STEPS], w2s,
                          start=True, stop=True)
            last.then_inc(mm_cond, 1)
            pe.wait_ge(dve_cond, 6)
            pe.wait_ge(consts, 3)
            for c in range(NC):
                mix(0, 0, 0, c)

            def step(j, par, lay, lay1, lay2):
                agate(j, par, lay)
                for k in range(KT):
                    base(j, par, lay, (k,))
                    if lay1 is not None and k in MIX_AFTER:
                        mix(j + (1 if par else 0), 1 - par, lay1, MIX_AFTER.index(k))
                    if k == TURN_AFTER:
                        turn(j, par)
                up(j, par, lay)

            run(pe, step)


_OUT = ((128, 64, 1024), "float32")


def kernel(**inputs):
    import numpy as np
    import concourse.bacc as bacc
    from concourse.bass_utils import run_bass_kernel_spmd

    a = {k: np.asarray(v) for k, v in inputs.items()}

    def rq(w):
        return w.reshape(*w.shape[:-1], Q, BR).swapaxes(-1, -2).reshape(w.shape)

    arrays = {
        "x": a["x"].reshape(-1, H),
        "condw": np.concatenate([
            a["L0_cond_W0"], a["cond_128"].reshape(-1, 2, 128).transpose(2, 1, 0).reshape(128, -1), a["L0_cond_W1"],
            a["L0_cond_W2"], a["L1_cond_c_weight"].T, a["L0_cond_b0"][:, None], a["L0_cond_b1"][:, None]], axis=1),
        "condr": np.concatenate([a["L0_cond_bias_k"].reshape(-1), a["L0_cond_b2"], a["fside_S_0"], a["L0_ffn_b_thr"]]),
        "mixw": a["L0_cond_weight"][..., 0].transpose(2, 0, 1),
        "l0wT": rq(a["L0_ffn_W_base"].T), "l0b": rq(a["L0_ffn_b_base"]),
        "l0ag": np.concatenate([a["L0_ffn_A"].reshape(ER, H), a["L0_ffn_W_gate"], a["L0_ffn_W_thr"]]).T,
        "l0B": rq(a["L0_ffn_B"].transpose(0, 2, 1).reshape(ER, H)),
        "convw": a["L1_cond_weight"].reshape(G, GC, GC, TAPS)[..., ::-1].transpose(2, 0, 3, 1),
        "l1wT": rq(a["L1_ffn_base_w"].T), "l1b": rq(a["L1_ffn_base_b"]),
        "l1ag": np.concatenate([a["L1_ffn_lora_A"].reshape(ER, H), a["L1_ffn_gate_w"]]).T,
        "l1B": rq(a["L1_ffn_lora_B"].transpose(0, 2, 1).reshape(ER, H)),
    }
    nc = bacc.Bacc("TRN2", target_bir_lowering=False, num_devices=1)
    feeds, args = {}, []
    for name, v in arrays.items():
        v = np.ascontiguousarray(v)
        feeds[f"in_{name}"] = v
        args.append(nc.dram_tensor(f"in_{name}", v.shape, mybir.dt.from_np(v.dtype), kind="ExternalInput").ap())
    out = nc.dram_tensor("out", (a["x"].shape[0] * C, H), F32, kind="ExternalOutput").ap()
    build(nc, *args, out)
    r = run_bass_kernel_spmd(nc, [feeds], core_ids=[0])
    return np.asarray(r.results[0]["out"]).reshape(_OUT[0])
```

```python
import concourse.bass as bass
from concourse import mybir
from contextlib import ExitStack

F32 = mybir.dt.float32
F32R = mybir.dt.float32r
U32 = mybir.dt.uint32
ALU = mybir.AluOpType
ACT = mybir.ActivationFunctionType
AX = mybir.AxisListType

P = 128
C = 64
H = 1024
KT = H // P
HB = 512
E_, R_ = 8, 16
ER = E_ * R_
NAG = (ER + E_ + 2, ER + E_)
G, GC = 4, 16
TAPS, PAD = 9, 4
BR = 8
Q = H // BR
EIGHTHS = ((0, 3), (3, 6), (6, 8))
BANK0 = tuple(a * H // BR for a, _ in EIGHTHS)
UP_EIGHTHS = (0, 1, 2, 6, 3, 4, 5, 7)
BANKN = tuple((b - a) * H // BR for a, b in EIGHTHS)
NW = H + NAG[0]
BG = P // GC
QP = Q + 1
XW = BG * QP
MODES = 8
MIX_AFTER = (1, 3, 4, 5)
TURN_AFTER, UP_AFTER = 2, 3
NC = 4
CH = H // NC


def bcast(ap, axis, n):
    v = ap.unsqueeze(axis)
    shape = list(v.shape)
    shape[axis] = n
    return v.broadcast_to(shape)


def build(nc, x, condw, condr, mixw, l0w, l0b, l0B, convw, l1w, l1b, l1B, out):
    NT = x.shape[0]
    STEPS = NT // P
    x1 = nc.dram_tensor("x1_scratch", [NT, H], F32).ap()
    rows = nc.dram_tensor("row_scratch", [2, STEPS, P], F32).ap()
    atts = nc.dram_tensor("att_scratch", [2, STEPS, MODES], F32).ap()

    with ExitStack() as ctx:
        def sb(name, shape, dt=F32):
            return ctx.enter_context(nc.sbuf_tensor(name, shape, dt))

        def sem(name):
            return ctx.enter_context(nc.semaphore(name))

        stage = sb("stage", [P, KT, NW])
        Whi, Wlo = sb("Whi", [P, KT, NW], F32R), sb("Wlo", [P, KT, NW], F32R)
        Bhi, Blo = sb("Bhi", [P, 2, H], F32R), sb("Blo", [P, 2, H], F32R)
        CT = sb("CT", [P, G, 2, 2, P], F32R)
        bias = sb("bias", [P, H])
        Xraw = sb("Xraw", [P, 2, XW])
        Xhi, Xlo = sb("Xhi", [P, XW], F32R), sb("Xlo", [P, XW], F32R)
        Y = sb("Y", [P, H])
        Yhi, Ylo = sb("Yhi", [P, 2, H], F32R), sb("Ylo", [P, 2, H], F32R)
        res = sb("res", [P, 2, H])
        outb = sb("outb", [P, 2, H])
        row = sb("row", [P, 2, P])
        attb = sb("attb", [P, STEPS, MODES])
        mixT = sb("mixT", [P, MODES, C])
        prod = sb("prod", [P, MODES, C])
        agg = sb("agg", [P, C])
        M = sb("M", [P, 2, P], F32R)
        ag = sb("ag", [P, NAG[0]])
        hw = sb("hw", [P, P])
        HThi, HTlo = sb("HThi", [P, P], F32R), sb("HTlo", [P, P], F32R)
        ident = sb("ident", [P, P])
        iota = sb("iota", [P, E_])
        small = sb("small", [P, 64])
        idx = sb("idx", [P, E_], U32)
        nmax, den, rec = small[:, 0:1], small[:, 2:4], small[:, 4:6]
        texp, wsum, guard, rguard = small[:, 6:7], small[:, 7:8], small[:, 8:9], small[:, 9:10]
        nbthr, m8 = small[:, 10:11], small[:, 16:24]
        eg, adapted, wrelu, wts = small[:, 24:32], small[:, 32:40], small[:, 40:48], small[:, 48:56]
        diff, idxf, e2, s2, r2 = small[:, 1:2], small[:, 56:58], small[:, 58:59], small[:, 59:60], small[:, 60:61]
        hot2, hot12 = small[:, 24:32], small[:, 32:40]

        psB = ctx.enter_context(nc.psum_tensor("psB", [P, 6, HB], F32))
        psT = ctx.enter_context(nc.psum_tensor("psT", [P, 2, HB], F32))
        psG, psW = psB[:, 0, :], psB[:, 1, :]

        def turned(par):
            return psB[:, 3 * par + 2, BANKN[2]:BANKN[2] + P]

        h0, h1 = Y[:, 0:P], Y[:, P:2 * P]
        conds = outb[:, 1, 0:condw.shape[1]]
        w0s, emb, w1s = (conds[:, k * P:(k + 1) * P] for k in range(3))
        w2s, cws = conds[:, 3 * P:3 * P + MODES], conds[:, 3 * P + MODES:3 * P + MODES + C]
        b0s, b1s = conds[:, 456:457], conds[:, 457:458]
        condrs = Y[:, 2 * P:2 * P + condr.shape[0]]
        mixbs = condrs[0:STEPS, 0:MODES * C].rearrange("p (k o) -> p k o", k=MODES)
        b2s, cbs = condrs[0:STEPS, 512:520], condrs[0:STEPS, 520:584]
        bthrs = condrs[:, 584:585]
        lg, ex, att = (Y[0:STEPS, k:k + 16].rearrange("p (a k) -> p a k", a=2) for k in (900, 916, 932))
        nmx2, sum2, rec2 = Y[0:STEPS, 948:950], Y[0:STEPS, 950:952], Y[0:STEPS, 952:954]
        aprod = outb[0:STEPS, 0, :].rearrange("p (a k o) -> p a k o", a=2, k=MODES)
        arow, crow = outb[0:STEPS, 1, 768:896], outb[0:STEPS, 1, 896:1024]
        flat = stage[:, KT - 2:KT, :].rearrange("p k n -> p (k n)")
        b1raw = flat[:, 0:H]
        craw = flat[:, H:H + G * 2 * P].rearrange("p (g w n) -> p g w n", g=G, w=2)
        b0raw = outb[:, 0, :]

        cond_in, condr_in, mix_in = sem("cond_in"), sem("condr_in"), sem("mix_in")
        b0_in, bias_in = sem("b0_in"), sem("bias_in")
        w_in = [sem(f"w_in{k}") for k in range(KT)]
        l1s_in, conv_zero, conv_in = sem("l1s_in"), sem("conv_zero"), sem("conv_in")
        ident_zero, consts = sem("ident_zero"), sem("consts")
        mm_cond, act_cond, dve_cond = sem("mm_cond"), sem("act_cond"), sem("dve_cond")
        cond_out, att_in = sem("cond_out"), sem("att_in")
        w_hi, w_lo, w_loP = sem("w_hi"), sem("w_lo"), sem("w_loP")
        s_hi, s_lo, s_loP = sem("s_hi"), sem("s_lo"), sem("s_loP")
        base_tile = sem("base_tile")
        x_loaded = [sem(f"x_loaded{p}") for p in range(2)]
        g_loaded = [sem(f"g_loaded{p}") for p in range(2)]
        r_loaded = [sem(f"r_loaded{p}") for p in range(2)]
        row_loaded = [sem(f"row_loaded{p}") for p in range(2)]
        stored = [sem(f"stored{p}") for p in range(2)]
        pad_zero = sem("pad_zero")
        x_hi, x_lo = sem("x_hi"), sem("x_lo")
        prod_ready, agg_ready, m_hi, m_lo = sem("prod_ready"), sem("agg_ready"), sem("m_hi"), sem("m_lo")
        mixed, y_part, y_chunk, yhi_half, ylo_half = sem("mixed"), sem("y_part"), sem("y_chunk"), sem("yhi_half"), sem("ylo_half")
        base_done, ag_copied = sem("base_done"), sem("ag_copied")
        nmax_ready, exp_ready, gate0 = sem("nmax_ready"), sem("exp_ready"), sem("gate0")
        m8_ready, diff_ready, exp2_ready, gate1 = sem("m8_ready"), sem("diff_ready"), sem("exp2_ready"), sem("gate1")
        hw_ready, tr_done, ht_hi, ht_lo = sem("hw_ready"), sem("tr_done"), sem("ht_hi"), sem("ht_lo")
        wts_ready, up_done = sem("wts_ready"), sem("up_done")
        res_ready, rest_added, o_done = sem("res_ready"), sem("rest_added"), sem("o_done")

        def as_f32(ap):
            return ap.bitcast(F32)

        def run(eng, step):
            def layer(n):
                return n // STEPS if 0 <= n < 2 * STEPS else None

            def peeled(n):
                step(n // 2, n % 2, *(layer(n + d) for d in (-1, 0, 1, 2)))

            for lay in range(2):
                first = lay * STEPS
                peeled(first)
                peeled(first + 1)
                with eng.Fori(first // 2 + 1, (first + STEPS) // 2 - 1) as j:
                    step(j, 0, lay, lay, lay, lay)
                    step(j, 1, lay, lay, lay, lay)
                peeled(first + STEPS - 2)
                peeled(first + STEPS - 1)

        def before(j, par):
            return (j, 0) if par else (j - 1, 1)

        def after(j, par):
            return (j + 1, 0) if par else (j, 1)

        block = ctx.enter_context(nc.Block())

        @block.sync
        def _(sp):
            def load_x(j, par, layer):
                n = 2 * j + par
                if layer == 0:
                    sp.dma_start(Xraw[:, par, 0:H], x[bass.ds(n * P, P), :]).then_inc(x_loaded[par], 16)
                else:
                    dst = Xraw[:, par, :].rearrange("p (b q) -> p b q", b=BG)
                    m = n - STEPS
                    src = x1[bass.ds(m * P, P), :].rearrange("(b i) (r q) -> r i b q", b=BG, r=BR)
                    for r in range(BR):
                        first = 1 if r < PAD else 0
                        sp.dma_start(dst[r * GC:(r + 1) * GC, :, first:first + Q], src[(r + PAD) % BR])\
                            .then_inc(g_loaded[par], 16)
                sp.dma_start(row[:, par, :], rows[layer, bass.ds(n - layer * STEPS, 1), :].rearrange("a t -> (a t)")
                             .partition_broadcast(P)).then_inc(row_loaded[par], 16)

            sp.dma_start(conds, condw).then_inc(cond_in, 16)
            sp.dma_start(Xraw[:, 0, 0:H], x[0:P, :]).then_inc(x_loaded[0], 16)

            def load_w(ks):
                for k in ks:
                    sp.dma_start(stage[:, k, 0:NW - 1], l0w[k * P:(k + 1) * P, :]).then_inc(w_in[k], 16)

            load_w(range(0, 1))
            sp.wait_ge(dve_cond, 4)
            sp.dma_start(atts.rearrange("a s k -> s a k"), att).then_inc(cond_out, 16)
            load_w(range(1, 2))
            sp.wait_ge(cond_out, 16)
            for a in range(2):
                sp.dma_start(attb[a * C:(a + 1) * C, :, :].rearrange("p s k -> p (s k)"),
                             atts[a].rearrange("s k -> (s k)").partition_broadcast(C)).then_inc(att_in, 16)
            sp.wait_ge(dve_cond, 6)
            sp.dma_start(rows[0], arow).then_inc(cond_out, 16)
            sp.dma_start(rows[1], crow).then_inc(cond_out, 16)
            load_w(range(2, 3))
            sp.wait_ge(cond_out, 48)
            for par in range(2):
                sp.dma_start(row[:, par, :], rows[0, par, :].partition_broadcast(P)).then_inc(row_loaded[par], 16)
            load_w(range(3, 5))
            sp.dma_start(Xraw[:, 1, 0:H], x[P:2 * P, :]).then_inc(x_loaded[1], 16)
            load_w(range(5, KT))
            sp.dma_start(b0raw, l0B).then_inc(b0_in, 16)
            sp.dma_start(bias[:, :], l0b.partition_broadcast(P)).then_inc(bias_in, 16)

            def step(j, par, lay0, lay, lay1, lay2):
                n = 2 * j + par
                if lay2 is not None:
                    sp.wait_ge(x_hi, n + 1)
                    sp.wait_ge(x_lo, n + 1)
                    if lay == 0:
                        sp.wait_ge(res_ready, n + 1)
                    sp.wait_ge(y_chunk, NC * n + NC)
                    if lay2 == 1:
                        if lay == 0:
                            sp.wait_ge(pad_zero, par + 1)
                        sp.wait_ge(stored[par], 16 * (j - STEPS // 2 + 2))
                    load_x(j + 1, par, lay2)
                if lay == 0 and isinstance(j, int) and n == 0:
                    sp.wait_ge(w_hi, KT)
                    sp.wait_ge(w_lo, KT // 2)
                    sp.wait_ge(w_loP, KT // 2)
                    sp.dma_start(b1raw, l1B).then_inc(l1s_in, 16)
                    sp.wait_ge(conv_zero, 1)
                    for r in range(BR):
                        to = craw[r * GC:(r + 1) * GC, :, :, :].rearrange("p g w (t o) -> p g w t o", o=GC)
                        sp.dma_start(to[:, :, 0, 0:r + 1, :], convw[:, :, BR - r:BR + 1, :]).then_inc(conv_in, 16)
                        sp.dma_start(to[:, :, 1, r:BR, :], convw[:, :, 0:BR - r, :]).then_inc(conv_in, 16)
                if isinstance(j, int) and n == STEPS - 1:
                    sp.dma_start(bias[:, :], l1b.partition_broadcast(P)).then_inc(bias_in, 16)
                if lay0 is not None:
                    store(*before(j, par), lay0)
                if isinstance(j, int) and n in (1, STEPS - 2):
                    if n > 1:
                        sp.wait_ge(s_hi, 3)
                        sp.wait_ge(s_loP, 2)
                    for k in range(0, KT // 2) if n == 1 else range(KT // 2, KT):
                        sp.dma_start(stage[:, k, 0:H + NAG[1]], l1w.rearrange("(p k) n -> p k n", p=P)[:, k, :])\
                            .then_inc(w_in[k], 16)
                if lay1 == 1:
                    sp.dma_start(res[:, 1 - par, :], x1[bass.ds((n + 1 - STEPS) * P, P), :])\
                        .then_inc(r_loaded[1 - par], 16)

            def store(j, par, layer):
                n = 2 * j + par
                sp.wait_ge(o_done, n + 1)
                to = x1 if layer == 0 else out
                sp.dma_start(to[bass.ds((n - layer * STEPS) * P, P), :], outb[:, par, :]).then_inc(stored[par], 16)

            run(sp, step)
            store(STEPS - 1, 1, 1)
            for par in range(2):
                sp.wait_ge(stored[par], 16 * STEPS)

        @block.gpsimd
        def _(pool):
            pool.memset(ident[:, :], 0.0).then_inc(ident_zero, 1)
            pool.wait_ge(ident_zero, 1)
            pool.affine_select(out=ident[:, :], in_=ident[:, :], compare_op=ALU.not_equal, fill=1.0, base=0,
                               pattern=[[-1, P]], channel_multiplier=1).then_inc(consts, 1)
            for e in range(E_):
                last = pool.memset(iota[:, e:e + 1], float(e))
            last.then_inc(consts, 1)
            pool.memset(as_f32(M[:, :, :]), 0.0)
            pool.memset(stage[:, :, NW - 1:NW], 0.0).then_inc(consts, 1)

            def split_lo(k, layer):
                pool.wait_ge(w_hi, KT * layer + k + 1)
                w = H + NAG[layer]
                pool.tensor_tensor(Wlo[:, k, 0:w], stage[:, k, 0:w], as_f32(Whi[:, k, 0:w]), ALU.subtract)\
                    .then_inc(w_loP, 1)

            def low_x(j, par, layer):
                n = 2 * j + par
                w = H if layer == 0 else XW
                pool.wait_ge(x_hi, n + 1)
                pool.tensor_tensor(Xlo[:, 0:w], Xraw[:, par, 0:w], as_f32(Xhi[:, 0:w]), ALU.subtract).then_inc(x_lo, 1)

            low_x(0, 0, 0)
            for k in range(1, KT // 2, 2):
                split_lo(k, 0)
            low_x(0, 1, 0)
            for k in range(KT // 2 + 1, KT, 2):
                split_lo(k, 0)
            pool.wait_ge(bias_in, 16)

            def residual(j, par, layer):
                n = 2 * j + par
                if layer == 0:
                    pool.wait_ge(x_loaded[par], 16 * (j + 1))
                    if not (isinstance(j, int) and j == 0):
                        pool.wait_ge(o_done, n - 1)
                    pool.tensor_tensor(res[:, par, :].rearrange("p (r q) -> p r q", r=BR),
                                       Xraw[:, par, 0:H].rearrange("p (q r) -> p r q", r=BR),
                                       bias[:, :].rearrange("p (r q) -> p r q", r=BR), ALU.add)\
                        .then_inc(res_ready, 1)
                else:
                    if isinstance(j, int) and n == STEPS:
                        pool.wait_ge(bias_in, 32)
                    pool.wait_ge(r_loaded[par], 16 * (j - STEPS // 2 + 1))
                    pool.tensor_tensor(res[:, par, :], res[:, par, :], bias[:, :], ALU.add).then_inc(res_ready, 1)

            residual(0, 0, 0)

            def step(j, par, lay0, lay, lay1, lay2):
                n = 2 * j + par
                if isinstance(j, int) and n == 0:
                    pool.wait_ge(w_hi, KT)
                    pool.wait_ge(w_lo, KT // 2)
                    pool.wait_ge(w_loP, KT // 2)
                    pool.memset(craw, 0.0).then_inc(conv_zero, 1)
                if isinstance(j, int) and n in (STEPS - 2, STEPS - 1):
                    pool.wait_ge(x_hi, n + 1)
                    pool.wait_ge(x_lo, n + 1)
                    pool.wait_ge(res_ready, n + 1)
                    v = Xraw[:, par, :].rearrange("p (b q) -> p b q", b=BG)
                    pool.memset(v[:, :, 0:QP:Q], 0.0).then_inc(pad_zero, 1)
                if isinstance(j, int) and n == STEPS - 1:
                    for k in range(1, KT - 2, 2):
                        split_lo(k, 1)
                if lay2 is not None:
                    low_x(j + 1, par, lay2)
                if isinstance(j, int) and n == STEPS - 1:
                    split_lo(KT - 1, 1)
                if lay1 is not None:
                    residual(*after(j, par), lay1)
                if isinstance(j, int) and n == 1:
                    pool.wait_ge(s_hi, 2)
                    pool.tensor_tensor(Blo[:, 1, :], b1raw, as_f32(Bhi[:, 1, :]), ALU.subtract).then_inc(s_loP, 1)
                    pool.wait_ge(s_hi, 3)
                    pool.tensor_tensor(CT[:, :, :, 1, :], craw, as_f32(CT[:, :, :, 0, :]), ALU.subtract)\
                        .then_inc(s_loP, 1)

            run(pool, step)

        @block.scalar
        def _(act):
            act.dma_start(condrs, condr.partition_broadcast(P)).then_inc(condr_in, 16)
            for a in range(2):
                act.dma_start(mixT[a * C:(a + 1) * C, :, :], mixw).then_inc(mix_in, 16)

            def high_x(j, par, layer):
                n = 2 * j + par
                if layer == 0:
                    act.wait_ge(x_loaded[par], 16 * (j + 1))
                    w = H
                else:
                    act.wait_ge(g_loaded[par], 16 * BR * (j - STEPS // 2 + 1))
                    w = XW
                if not (isinstance(n, int) and n == 0):
                    act.wait_ge(mixed, NC * n)
                nc.scalar.copy(Xhi[:, 0:w], Xraw[:, par, 0:w]).then_inc(x_hi, 1)

            def high_m(n):
                act.wait_ge(agg_ready, n + 1)
                nc.scalar.copy(M[0:C, 0, 0:C], agg[0:C, :])
                nc.scalar.copy(M[C:P, 0, C:P], agg[C:P, :]).then_inc(m_hi, 1)

            def split_y(j, par, layer):
                n = 2 * j + par
                if not (isinstance(j, int) and j == 0):
                    act.wait_ge(base_done, n - 1)
                for h in range(2):
                    act.wait_ge(y_chunk, NC * n + (2 * h + 2 if layer == 0 else NC))
                    nc.scalar.copy(Yhi[:, par, h * HB:(h + 1) * HB], Y[:, h * HB:(h + 1) * HB])\
                        .then_inc(yhi_half, 1)

            def split_w(k, layer):
                act.wait_ge(w_in[k], 16 * (layer + 1))
                if layer:
                    if k < KT - 1:
                        act.wait_ge(base_tile, k + 1)
                    else:
                        act.wait_ge(base_done, STEPS)
                w = H + NAG[layer]
                nc.scalar.copy(Whi[:, k, 0:w], stage[:, k, 0:w]).then_inc(w_hi, 1)

            act.wait_ge(mm_cond, 1)
            nc.scalar.activation(h0, psG[:, 0:P], ACT.Gelu, bias=b0s).then_inc(act_cond, 1)
            act.wait_ge(mm_cond, 3)
            nc.scalar.activation(h1, psW[:, 0:P], ACT.Gelu, bias=b1s).then_inc(act_cond, 1)
            high_x(0, 0, 0)
            act.wait_ge(dve_cond, 2)
            for a in range(2):
                nc.scalar.activation(ex[:, a, :], lg[:, a, :], ACT.Exp, bias=nmx2[:, a:a + 1],
                                     accum_out=sum2[:, a:a + 1]).then_inc(act_cond, 1)
            act.wait_ge(consts, 3)
            for k in range(2):
                split_w(k, 0)
            high_m(0)
            for k in range(2, KT // 2):
                split_w(k, 0)
            split_y(0, 0, 0)
            high_x(0, 1, 0)
            high_m(1)
            for k in range(KT // 2, KT):
                split_w(k, 0)
            act.wait_ge(b0_in, 16)
            nc.scalar.copy(Bhi[:, 0, :], b0raw).then_inc(s_hi, 1)

            def step(j, par, lay0, lay, lay1, lay2):
                n = 2 * j + par
                if lay0 is not None:
                    weigh(*before(j, par), lay0)
                if isinstance(j, int) and n == STEPS - 1:
                    for k in range(KT - 2):
                        split_w(k, 1)
                if lay1 is not None:
                    split_y(*after(j, par), lay1)
                if lay2 is not None:
                    high_x(j + 1, par, lay2)
                    if lay2 == 0:
                        high_m(n + 2)
                if isinstance(j, int) and n == 1:
                    act.wait_ge(l1s_in, 16)
                    nc.scalar.copy(Bhi[:, 1, :], b1raw).then_inc(s_hi, 1)
                    act.wait_ge(conv_in, 16 * 2 * BR)
                    nc.scalar.copy(CT[:, :, :, 0, :], craw).then_inc(s_hi, 1)
                if isinstance(j, int) and n == STEPS - 1:
                    for k in range(KT - 2, KT):
                        split_w(k, 1)

            def weigh(j, par, layer):
                n = 2 * j + par
                if layer == 0:
                    act.wait_ge(nmax_ready, n + 1)
                    nc.scalar.activation(eg, ag[:, ER:ER + E_], ACT.Exp, bias=nmax, accum_out=den[:, 0:1])
                    nc.scalar.activation(texp, ag[:, ER + E_:ER + E_ + 1], ACT.Exp, bias=nbthr, scale=-1.0)\
                        .then_inc(exp_ready, 1)
                else:
                    act.wait_ge(diff_ready, n - STEPS + 1)
                    nc.scalar.activation(e2, diff, ACT.Exp).then_inc(exp2_ready, 1)
                act.wait_ge(tr_done, n + 1)
                nc.scalar.copy(HThi[:, :], turned(par)).then_inc(ht_hi, 1)

            run(act, step)
            weigh(STEPS - 1, 1, 1)

        @block.vector
        def _(dve):
            def mixing_matrix(n):
                nc.vector.tensor_tensor(prod[:, :, :], mixT[:, :, :], bcast(attv(n), 2, C), ALU.mult)\
                    .then_inc(prod_ready, 1)
                dve.wait_ge(prod_ready, n + 1)
                if not (isinstance(n, int) and n == 0):
                    dve.wait_ge(m_hi, n)
                nc.vector.tensor_reduce(agg[:, :], prod[:, :, :].rearrange("p k o -> p o k"), AX.X, ALU.add)\
                    .then_inc(agg_ready, 1)

            def low_m(n):
                dve.wait_ge(agg_ready, n + 1)
                dve.wait_ge(m_hi, n + 1)
                nc.vector.tensor_tensor(M[0:C, 1, 0:C], agg[0:C, :], as_f32(M[0:C, 0, 0:C]), ALU.subtract)
                nc.vector.tensor_tensor(M[C:P, 1, C:P], agg[C:P, :], as_f32(M[C:P, 0, C:P]), ALU.subtract)\
                    .then_inc(m_lo, 1)

            def attv(n):
                if isinstance(n, int):
                    return attb[:, n, :]
                return attb[:, bass.ds(n, 1), :].rearrange("p a k -> p (a k)")

            def evacuate_y(j, par, layer, chunks):
                n = 2 * j + par
                if 0 in chunks:
                    dve.wait_ge(row_loaded[par], 16 * (j + 1))
                for c in chunks:
                    h = c // 2
                    dve.wait_ge(mixed, NC * n + c + 1)
                    if not (isinstance(n, int) and n == 0):
                        dve.wait_ge(yhi_half, 2 * n + (h - 1 if layer == 0 else 0))
                    bank = psT[:, c % 2, :].rearrange("p (b s n) -> p b s n", b=2, s=2)
                    if layer == 0:
                        y = Y[:, c * CH:(c + 1) * CH].rearrange("p (b n) -> p b n", b=2)
                        add = bcast(row[:, par, :], 1, 2)
                        parts = (bank[:, :, 0, :], bank[:, :, 1, :])
                    else:
                        y = Y[:, :].rearrange("p (t b o) -> p b t o", t=BR, b=BG)[:, 2 * c:2 * c + 2]
                        add = bcast(row[:, par, c * 2 * GC:(c + 1) * 2 * GC].rearrange("p (b o) -> p b o", b=2), 2, BR)
                        parts = tuple(bank[:, :, s, :].rearrange("p b (t o) -> p b t o", t=BR) for s in range(2))
                    nc.vector.tensor_tensor(y, parts[0], add, ALU.add).then_inc(y_part, 1)
                    dve.wait_ge(y_part, NC * n + c + 1)
                    nc.vector.tensor_tensor(y, parts[1], y, ALU.add).then_inc(y_chunk, 1)

            def split_y(j, par, layer):
                n = 2 * j + par
                for h in range(2):
                    dve.wait_ge(y_chunk, NC * n + (2 * h + 2 if layer == 0 else NC))
                    dve.wait_ge(yhi_half, 2 * n + h + 1)
                    nc.vector.tensor_tensor(Ylo[:, par, h * HB:(h + 1) * HB], Y[:, h * HB:(h + 1) * HB],
                                            as_f32(Yhi[:, par, h * HB:(h + 1) * HB]), ALU.subtract)\
                        .then_inc(ylo_half, 1)

            def split_w(k, layer):
                dve.wait_ge(w_hi, KT * layer + k + 1)
                w = H + NAG[layer]
                nc.vector.tensor_tensor(Wlo[:, k, 0:w], stage[:, k, 0:w], as_f32(Whi[:, k, 0:w]), ALU.subtract)\
                    .then_inc(w_lo, 1)

            def emit(j, par, layer):
                n = 2 * j + par
                r0, r1 = EIGHTHS[2]
                rest = res[:, par, r0 * Q:r1 * Q]
                dve.wait_ge(res_ready, n + 1)
                nc.vector.tensor_tensor(rest, psB[:, 3 * par + 2, 0:BANKN[2]], rest, ALU.add).then_inc(rest_added, 1)
                dve.wait_ge(up_done, n + 1)
                dve.wait_ge(rest_added, n + 1)
                if not (isinstance(j, int) and j == 0):
                    dve.wait_ge(stored[par], 16 * j)
                to = outb[:, par, :].rearrange("p (r q) -> p r q" if layer == 0 else "p (q r) -> p r q", r=BR)
                for b, (r0, r1) in enumerate(EIGHTHS):
                    if b < 2:
                        product = psB[:, 3 * par + b, 0:BANKN[b]].rearrange("p (r q) -> p r q", q=Q)
                    else:
                        product = psB[:, 3 * par:3 * par + 2, BANKN[0]:HB]
                    last = nc.vector.tensor_tensor(
                        to[:, r0:r1, :], product,
                        res[:, par, :].rearrange("p (r q) -> p r q", r=BR)[:, r0:r1, :], ALU.add)
                last.then_inc(o_done, 1)

            dve.wait_ge(condr_in, 16)
            dve.wait_ge(mm_cond, 4)
            nc.vector.tensor_tensor(lg, psG[0:STEPS, 128:144].rearrange("p (a k) -> p a k", a=2),
                                    bcast(b2s[:, 0:E_], 1, 2), ALU.add).then_inc(dve_cond, 1)
            dve.wait_ge(dve_cond, 1)
            nc.vector.tensor_reduce(nmx2, lg, AX.X, ALU.max, negate=True).then_inc(dve_cond, 1)
            dve.wait_ge(act_cond, 4)
            nc.vector.reciprocal(rec2, sum2).then_inc(dve_cond, 1)
            dve.wait_ge(dve_cond, 3)
            nc.vector.tensor_tensor(att, ex, bcast(rec2, 2, MODES), ALU.mult).then_inc(dve_cond, 1)
            dve.wait_ge(dve_cond, 4)
            for a in range(2):
                last = nc.vector.tensor_tensor(aprod[:, a], mixbs, bcast(att[:, a, :], 2, C), ALU.mult)
            last.then_inc(dve_cond, 1)
            dve.wait_ge(dve_cond, 5)
            for a in range(2):
                nc.vector.tensor_reduce(arow[:, a * C:(a + 1) * C], aprod[:, a].rearrange("p k o -> p o k"),
                                        AX.X, ALU.add)
            nc.vector.tensor_tensor(crow.rearrange("p (a o) -> p a o", a=2),
                                    psT[0:STEPS, 0, 0:P].rearrange("p (a o) -> p a o", a=2),
                                    bcast(cbs, 1, 2), ALU.add).then_inc(dve_cond, 1)
            nc.vector.tensor_scalar(nbthr, bthrs, -1.0, None, ALU.mult).then_inc(dve_cond, 1)
            dve.wait_ge(att_in, 32)
            dve.wait_ge(mix_in, 32)
            mixing_matrix(0)
            low_m(0)
            split_w(0, 0)
            evacuate_y(0, 0, 0, range(NC))
            split_y(0, 0, 0)
            mixing_matrix(1)
            split_w(2, 0)
            low_m(1)
            for k in range(KT // 2, KT, 2):
                split_w(k, 0)
            dve.wait_ge(s_hi, 1)
            nc.vector.tensor_tensor(Blo[:, 0, :], b0raw, as_f32(Bhi[:, 0, :]), ALU.subtract).then_inc(s_lo, 1)

            def gates0(j, par, logits):
                n = 2 * j + par
                g = 6 * n
                nc.vector.tensor_reduce(nmax, logits, AX.X, ALU.max, negate=True).then_inc(nmax_ready, 1)
                dve.wait_ge(exp_ready, n + 1)
                nc.vector.tensor_scalar(den[:, 1:2], texp, 1.0, 8.0, ALU.add, ALU.mult).then_inc(gate0, 1)
                dve.wait_ge(gate0, g + 1)
                nc.vector.reciprocal(rec, den).then_inc(gate0, 1)
                dve.wait_ge(gate0, g + 2)
                nc.vector.tensor_scalar(adapted, eg, rec[:, 0:1], rec[:, 1:2], ALU.mult, ALU.subtract)\
                    .then_inc(gate0, 1)
                dve.wait_ge(gate0, g + 3)
                nc.vector.tensor_scalar(wrelu, adapted, 0.0, 0.0, ALU.max, ALU.add, accum_out=wsum).then_inc(gate0, 1)
                dve.wait_ge(gate0, g + 4)
                nc.vector.scalar_tensor_tensor(guard, wsum, 0.0, wsum, ALU.is_equal, ALU.add).then_inc(gate0, 1)
                dve.wait_ge(gate0, g + 5)
                nc.vector.reciprocal(rguard, guard).then_inc(gate0, 1)
                dve.wait_ge(gate0, g + 6)
                return nc.vector.tensor_scalar(wts, wrelu, rguard, 2.0, ALU.mult, ALU.mult)

            def gates1(j, par, logits):
                n = 2 * j + par - STEPS
                g = 6 * n
                nc.vector.max(m8, logits).then_inc(m8_ready, 1)
                dve.wait_ge(m8_ready, n + 1)
                nc.vector.tensor_tensor(diff, m8[:, 1:2], m8[:, 0:1], ALU.subtract).then_inc(diff_ready, 1)
                nc.vector.max_index(idx[:, :], m8, logits).then_inc(gate1, 1)
                dve.wait_ge(gate1, g + 1)
                nc.vector.tensor_copy(idxf, idx[:, 0:2]).then_inc(gate1, 1)
                dve.wait_ge(exp2_ready, n + 1)
                nc.vector.tensor_scalar(s2, e2, 1.0, None, ALU.add).then_inc(gate1, 1)
                dve.wait_ge(gate1, g + 3)
                nc.vector.reciprocal(r2, s2).then_inc(gate1, 1)
                nc.vector.tensor_scalar(hot2, iota[:, :], idxf[:, 1:2], e2, ALU.is_equal, ALU.mult).then_inc(gate1, 1)
                dve.wait_ge(gate1, g + 5)
                nc.vector.scalar_tensor_tensor(hot12, iota[:, :], idxf[:, 0:1], hot2, ALU.is_equal, ALU.add)\
                    .then_inc(gate1, 1)
                dve.wait_ge(gate1, g + 6)
                return nc.vector.tensor_scalar(wts, hot12, r2, 2.0, ALU.mult, ALU.mult)

            def weigh(j, par, layer):
                n = 2 * j + par
                w = NAG[layer]
                bank = psB[:, 3 * par + 2, BANKN[2]:BANKN[2] + w]
                dve.wait_ge(base_done, n + 1)
                nc.vector.tensor_copy(ag[:, 0:w], bank).then_inc(ag_copied, 1)
                (gates0 if layer == 0 else gates1)(j, par, bank[:, ER:ER + E_]).then_inc(wts_ready, 1)
                dve.wait_ge(wts_ready, n + 1)
                dve.wait_ge(ag_copied, n + 1)
                if not (isinstance(n, int) and n == 0):
                    dve.wait_ge(tr_done, n)
                nc.vector.tensor_tensor(hw[:, :].rearrange("p (e r) -> p e r", e=E_),
                                        ag[:, 0:ER].rearrange("p (e r) -> p e r", e=E_),
                                        bcast(wts, 2, R_), ALU.mult).then_inc(hw_ready, 1)

            def low_ht(j, par):
                n = 2 * j + par
                dve.wait_ge(ht_hi, n + 1)
                nc.vector.tensor_tensor(HTlo[:, :], turned(par), as_f32(HThi[:, :]), ALU.subtract).then_inc(ht_lo, 1)

            def step(j, par, lay0, lay, lay1, lay2):
                n = 2 * j + par
                if lay0 is not None:
                    weigh(*before(j, par), lay0)
                if isinstance(j, int) and n == STEPS:
                    split_w(KT - 2, 1)
                if lay1 is not None:
                    evacuate_y(*after(j, par), lay1, range(0, 1))
                if lay0 is not None:
                    low_ht(*before(j, par))
                if isinstance(j, int) and n == STEPS - 1:
                    split_w(0, 1)
                if lay2 == 0:
                    mixing_matrix(n + 2)
                if lay1 is not None:
                    evacuate_y(*after(j, par), lay1, range(1, 2))
                if lay0 is not None:
                    emit(*before(j, par), lay0)
                if isinstance(j, int) and n == STEPS - 1:
                    split_w(2, 1)
                if lay1 is not None:
                    evacuate_y(*after(j, par), lay1, range(2, NC))
                    split_y(*after(j, par), lay1)
                if lay2 == 0:
                    low_m(n + 2)
                if isinstance(j, int) and n == STEPS - 1:
                    split_w(4, 1)

            run(dve, step)
            weigh(STEPS - 1, 1, 1)
            low_ht(STEPS - 1, 1)
            emit(STEPS - 1, 1, 1)

        @block.tensor
        def _(pe):
            mm = nc.tensor.matmul

            def mix(j, par, layer, c):
                n = 2 * j + par
                if c == 0:
                    pe.wait_ge(x_hi, n + 1)
                    pe.wait_ge(x_lo, n + 1)
                    if layer == 0:
                        pe.wait_ge(m_hi, n + 1)
                        pe.wait_ge(m_lo, n + 1)
                    elif isinstance(j, int) and n == STEPS:
                        pe.wait_ge(s_hi, 3)
                        pe.wait_ge(s_loP, 2)
                if not (isinstance(n, int) and n == 0 and c < 2):
                    pe.wait_ge(y_chunk, NC * n + c - 1)
                for t in range(2):
                    to = psT[:, c % 2, t * 2 * P:(t + 1) * 2 * P]
                    k = 2 * c + t
                    if layer == 0:
                        xs = slice(k * P, (k + 1) * P)
                        mm(to, Xhi[:, xs], M[:, :, :].rearrange("p s n -> p (s n)"), start=True, stop=False)
                        last = mm(to[:, 0:P], Xlo[:, xs], M[:, 0, :], start=False, stop=True)
                    else:
                        g = k % G
                        for w in range(2):
                            xs = slice(k * QP + w, k * QP + w + Q)
                            mm(to, Xhi[:, xs], CT[:, g, w, :, :].rearrange("p s n -> p (s n)"),
                               start=(w == 0), stop=False)
                            last = mm(to[:, 0:P], Xlo[:, xs], CT[:, g, w, 0, :], start=False, stop=(w == 1))
                last.then_inc(mixed, 1)

            def base(j, par, layer, k):
                n = 2 * j + par
                if k % (KT // 2) == 0:
                    pe.wait_ge(yhi_half, 2 * n + 1 + 2 * k // KT)
                    pe.wait_ge(ylo_half, 2 * n + 1 + 2 * k // KT)
                if k == 0 and not (isinstance(j, int) and j == 0):
                    pe.wait_ge(o_done, n - 1)
                if isinstance(j, int) and n in (0, STEPS):
                    pe.wait_ge(w_hi, KT * layer + k + 1)
                    pe.wait_ge(w_loP if k % 2 else w_lo, KT // 2 * layer + k // 2 + 1)
                yh, yl = Yhi[:, par, k * P:(k + 1) * P], Ylo[:, par, k * P:(k + 1) * P]
                for y, w in ((yh, Whi), (yh, Wlo), (yl, Whi)):
                    for b in range(3):
                        cols = BANKN[b] + (NAG[layer] if b == 2 else 0)
                        last = mm(psB[:, 3 * par + b, 0:cols], y, w[:, k, BANK0[b]:BANK0[b] + cols],
                                  start=(k == 0 and y is yh and w is Whi), stop=(b == 2 and k == KT - 1 and y is yl))
                if isinstance(j, int) and n == STEPS - 1 and k < KT - 1:
                    last.then_inc(base_tile, 1)
                if k == KT - 1:
                    last.then_inc(base_done, 1)

            def turn(j, par):
                n = 2 * j + par
                pe.wait_ge(hw_ready, n + 1)
                if isinstance(n, int) and n == 0:
                    pe.wait_ge(consts, 1)
                mm(turned(par), hw[:, :], ident[:, :], start=True, stop=True, is_transpose=True).then_inc(tr_done, 1)

            def up(j, par, layer):
                n = 2 * j + par
                if isinstance(n, int) and n == 0:
                    pe.wait_ge(s_hi, 1)
                    pe.wait_ge(s_lo, 1)
                pe.wait_ge(ht_hi, n + 1)
                pe.wait_ge(ht_lo, n + 1)
                for y, w in ((HThi, Bhi), (HThi, Blo), (HTlo, Bhi)):
                    for b in range(2):
                        for c0, c1 in ((0, BANKN[b]), (BANKN[b], HB)) if y is HThi and w is Bhi else ((0, HB),):
                            last = mm(psB[:, 3 * par + b, c0:c1], y[:, :], w[:, layer, b * HB + c0:b * HB + c1],
                                      start=False, stop=(y is HTlo))
                last.then_inc(up_done, 1)

            pe.wait_ge(cond_in, 16)
            mm(psG[:, 0:P], w0s, emb, start=True, stop=True).then_inc(mm_cond, 1)
            for a in range(2):
                last = mm(psT[0:STEPS, 0, a * C:(a + 1) * C], emb[:, a * STEPS:(a + 1) * STEPS], cws,
                          start=True, stop=True)
            last.then_inc(mm_cond, 1)
            pe.wait_ge(act_cond, 1)
            mm(psW[:, 0:P], w1s, h0, start=True, stop=True).then_inc(mm_cond, 1)
            pe.wait_ge(act_cond, 2)
            for a in range(2):
                last = mm(psG[0:STEPS, 128 + a * E_:128 + (a + 1) * E_], h1[:, a * STEPS:(a + 1) * STEPS], w2s,
                          start=True, stop=True)
            last.then_inc(mm_cond, 1)
            pe.wait_ge(dve_cond, 6)
            pe.wait_ge(consts, 3)
            for c in range(NC):
                mix(0, 0, 0, c)

            def step(j, par, lay0, lay, lay1, lay2):
                for k in range(KT):
                    base(j, par, lay, k)
                    if k == TURN_AFTER and lay0 is not None:
                        turn(*before(j, par))
                    if k in MIX_AFTER and lay1 is not None:
                        mix(*after(j, par), lay1, MIX_AFTER.index(k))
                    if k == UP_AFTER and lay0 is not None:
                        up(*before(j, par), lay0)

            run(pe, step)
            turn(STEPS - 1, 1)
            up(STEPS - 1, 1, 1)


_OUT = ((128, 64, 1024), "float32")


def kernel(**inputs):
    import numpy as np
    import concourse.bacc as bacc
    from concourse.bass_utils import run_bass_kernel_spmd

    a = {k: np.asarray(v) for k, v in inputs.items()}

    def rq(w):
        return w.reshape(*w.shape[:-1], Q, BR).swapaxes(-1, -2).reshape(w.shape)

    def up(w):
        return rq(w).reshape(ER, BR, Q)[:, UP_EIGHTHS, :].reshape(ER, H)

    arrays = {
        "x": a["x"].reshape(-1, H),
        "condw": np.concatenate([
            a["L0_cond_W0"], a["cond_128"].reshape(-1, 2, 128).transpose(2, 1, 0).reshape(128, -1), a["L0_cond_W1"],
            a["L0_cond_W2"], a["L1_cond_c_weight"].T, a["L0_cond_b0"][:, None], a["L0_cond_b1"][:, None]], axis=1),
        "condr": np.concatenate([a["L0_cond_bias_k"].reshape(-1), a["L0_cond_b2"], a["fside_S_0"], a["L0_ffn_b_thr"]]),
        "mixw": a["L0_cond_weight"][..., 0].transpose(2, 0, 1),
        "l0w": np.concatenate([rq(a["L0_ffn_W_base"].T), a["L0_ffn_A"].reshape(ER, H).T, a["L0_ffn_W_gate"].T,
                               a["L0_ffn_W_thr"].T], axis=1),
        "l0b": rq(a["L0_ffn_b_base"]),
        "l0B": up(a["L0_ffn_B"].transpose(0, 2, 1).reshape(ER, H)),
        "convw": a["L1_cond_weight"].reshape(G, GC, GC, TAPS)[..., ::-1].transpose(2, 0, 3, 1),
        "l1w": np.concatenate([rq(a["L1_ffn_base_w"].T), a["L1_ffn_lora_A"].reshape(ER, H).T,
                               a["L1_ffn_gate_w"].T], axis=1),
        "l1b": rq(a["L1_ffn_base_b"]),
        "l1B": up(a["L1_ffn_lora_B"].transpose(0, 2, 1).reshape(ER, H)),
    }
    nc = bacc.Bacc("TRN2", target_bir_lowering=False, num_devices=1)
    feeds, args = {}, []
    for name, v in arrays.items():
        v = np.ascontiguousarray(v)
        feeds[f"in_{name}"] = v
        args.append(nc.dram_tensor(f"in_{name}", v.shape, mybir.dt.from_np(v.dtype), kind="ExternalInput").ap())
    out = nc.dram_tensor("out", (a["x"].shape[0] * C, H), F32, kind="ExternalOutput").ap()
    build(nc, *args, out)
    r = run_bass_kernel_spmd(nc, [feeds], core_ids=[0])
    return np.asarray(r.results[0]["out"]).reshape(_OUT[0])
```
